# Optimizing a Trainium2 kernel written in Bass

```python
import numpy as np
import jax
import jax.numpy as jnp

def _softmax(x, axis=-1):
    return jax.nn.softmax(x, axis=axis)

def _gelu(x):
    return jax.nn.gelu(x, approximate=True)

def _silu(x):
    return jax.nn.silu(x)

def _sigmoid(x):
    return jax.nn.sigmoid(x)

def _layernorm(x, axis=-1, eps=1e-05):
    m = jnp.mean(x, axis=axis, keepdims=True)
    v = jnp.var(x, axis=axis, keepdims=True)
    return (x - m) / jnp.sqrt(v + eps)

def _scatter_add(tgt, idx, src, axis=0):
    return tgt.at[idx].add(src)

def _segment_sum(src, seg, n):
    return jax.ops.segment_sum(src, seg, n)
kernel_name = 'mk_recurrent_d2_jaxref_r8_238762'

def setup_inputs(seed: int=0):
    np.random.seed(seed)
    _w = jnp.asarray

    def _L0_attn_setup():
        import jax, jax.numpy as jnp
        import numpy as np
        NEG = 10000.0
        key = jax.random.key(seed)
        ks = jax.random.split(key, 5)
        B, S, D = (2, 256, 128)
        std = 1.0 / np.sqrt(D)
        return {'x': jax.random.normal(ks[0], (B, S, D), dtype=jnp.float32), 'Wq': jax.random.normal(ks[1], (D, D), dtype=jnp.float32) * std, 'bq': jnp.zeros((D,), jnp.float32), 'Wk': jax.random.normal(ks[2], (D, D), dtype=jnp.float32) * std, 'bk': jnp.zeros((D,), jnp.float32), 'Wv': jax.random.normal(ks[3], (D, D), dtype=jnp.float32) * std, 'bv': jnp.zeros((D,), jnp.float32), 'Wo': jax.random.normal(ks[4], (D, D), dtype=jnp.float32) * std, 'bo': jnp.zeros((D,), jnp.float32)}
    _L0_attn_in = _L0_attn_setup()

    def _L0_ffn_setup():
        import jax, jax.numpy as jnp
        import numpy as np
        D_MODEL, D_FF, N_EXP = (128, 512, 8)
        key = jax.random.key(seed)
        ks = jax.random.split(key, 8)
        s = lambda fan_in: 1.0 / np.sqrt(fan_in)
        x = jax.random.normal(ks[0], (4, 256, D_MODEL), dtype=jnp.float32)
        Wr = jax.random.uniform(ks[1], (N_EXP, D_MODEL), jnp.float32, -s(D_MODEL), s(D_MODEL))
        br = jax.random.uniform(ks[2], (N_EXP,), jnp.float32, -s(D_MODEL), s(D_MODEL))
        W1 = jax.random.uniform(ks[3], (N_EXP, D_FF, D_MODEL), jnp.float32, -s(D_MODEL), s(D_MODEL))
        b1 = jax.random.uniform(ks[4], (N_EXP, D_FF), jnp.float32, -s(D_MODEL), s(D_MODEL))
        W2 = jax.random.uniform(ks[5], (N_EXP, D_MODEL, D_FF), jnp.float32, -s(D_FF), s(D_FF))
        b2 = jax.random.uniform(ks[6], (N_EXP, D_MODEL), jnp.float32, -s(D_FF), s(D_FF))
        return {'x': x, 'Wr': Wr, 'br': br, 'W1': W1, 'b1': b1, 'W2': W2, 'b2': b2}
    _L0_ffn_in = _L0_ffn_setup()

    def _L1_attn_setup():
        import jax, jax.numpy as jnp
        import numpy as np
        D_MODEL = 128
        N_HEADS = 16
        HEAD_DIM = D_MODEL // N_HEADS
        BATCH = 2
        SEQ = 256

        def _alibi_bias(seq_len, n_heads, dtype):
            slopes = 1.0 / 2.0 ** (jnp.arange(n_heads, dtype=dtype) / n_heads)
            rel = jnp.arange(seq_len, dtype=dtype)[None, :] - jnp.arange(seq_len, dtype=dtype)[:, None]
            return slopes[:, None, None] * rel[None, :, :]
        key = jax.random.key(seed)
        ks = jax.random.split(key, 9)
        s = 0.02
        return {'x': jax.random.normal(ks[0], (BATCH, SEQ, D_MODEL), dtype=jnp.float32), 'Wq': jax.random.normal(ks[1], (D_MODEL, D_MODEL), dtype=jnp.float32) * s, 'bq': jnp.zeros((D_MODEL,), dtype=jnp.float32), 'Wk': jax.random.normal(ks[2], (D_MODEL, D_MODEL), dtype=jnp.float32) * s, 'bk': jnp.zeros((D_MODEL,), dtype=jnp.float32), 'Wv': jax.random.normal(ks[3], (D_MODEL, D_MODEL), dtype=jnp.float32) * s, 'bv': jnp.zeros((D_MODEL,), dtype=jnp.float32), 'Wo': jax.random.normal(ks[4], (D_MODEL, D_MODEL), dtype=jnp.float32) * s, 'bo': jnpp_zeros() if False else jnp.zeros((D_MODEL,), dtype=jnp.float32)}
    _L1_attn_in = _L1_attn_setup()

    def _L1_ffn_setup():
        import jax, jax.numpy as jnp
        import numpy as np
        B, S, H = (2, 256, 128)
        F = 512
        E = 8
        TOP_K = 2
        SHARED_SCALE = 0.1
        EPS = 1e-09

        def _moe_forward(x3, Wg, W1, b1, W2, b2, Ws1, bs1, Ws2, bs2):
            b, s, h = x3.shape
            x = x3.reshape(-1, h)
            T = x.shape[0]
            logits = x @ Wg
            probs = jax.nn.softmax(logits, axis=-1)
            vals, idx = jax.lax.top_k(probs, TOP_K)
            weights = vals / (jnp.sum(vals, axis=-1, keepdims=True) + EPS)
            cw = jnp.zeros((T, E), dtype=x.dtype).at[jnp.arange(T)[:, None], idx].set(weights)
            hpre = jnp.einsum('th,ehf->tef', x, W1) + b1
            act = jax.nn.silu(hpre)
            y = jnp.einsum('tef,efh->teh', act, W2) + b2
            out = jnp.einsum('te,teh->th', cw, y)
            shared = jax.nn.silu(x @ Ws1 + bs1) @ Ws2 + bs2
            out = out + SHARED_SCALE * shared
            return out.reshape(b, s, h)
        key = jax.random.key(seed)
        ks = jax.random.split(key, 10)
        sc = 0.02
        return {'hidden_states': jax.random.normal(ks[0], (B, S, H), dtype=jnp.float32), 'Wg': jax.random.normal(ks[1], (H, E), dtype=jnp.float32) * sc, 'W1': jax.random.normal(ks[2], (E, H, F), dtype=jnp.float32) * sc, 'b1': jnp.zeros((E, F), dtype=jnp.float32), 'W2': jax.random.normal(ks[3], (E, F, H), dtype=jnp.float32) * sc, 'b2': jnp.zeros((E, H), dtype=jnp.float32), 'Ws1': jax.random.normal(ks[4], (H, F), dtype=jnp.float32) * sc, 'bs1': jnp.zeros((F,), dtype=jnp.float32), 'Ws2': jax.random.normal(ks[5], (F, H), dtype=jnp.float32) * sc, 'bs2': jnp.zeros((H,), dtype=jnp.float32)}
    _L1_ffn_in = _L1_ffn_setup()
    _d = {'L0_attn_x': _L0_attn_in['x'], 'L0_attn_Wq': _L0_attn_in['Wq'], 'L0_attn_bq': _L0_attn_in['bq'], 'L0_attn_Wk': _L0_attn_in['Wk'], 'L0_attn_bk': _L0_attn_in['bk'], 'L0_attn_Wv': _L0_attn_in['Wv'], 'L0_attn_bv': _L0_attn_in['bv'], 'L0_attn_Wo': _L0_attn_in['Wo'], 'L0_attn_bo': _L0_attn_in['bo'], 'L0_ffn_Wr': _L0_ffn_in['Wr'], 'L0_ffn_br': _L0_ffn_in['br'], 'L0_ffn_W1': _L0_ffn_in['W1'], 'L0_ffn_b1': _L0_ffn_in['b1'], 'L0_ffn_W2': _L0_ffn_in['W2'], 'L0_ffn_b2': _L0_ffn_in['b2'], 'L1_attn_Wq': _L1_attn_in['Wq'], 'L1_attn_bq': _L1_attn_in['bq'], 'L1_attn_Wk': _L1_attn_in['Wk'], 'L1_attn_bk': _L1_attn_in['bk'], 'L1_attn_Wv': _L1_attn_in['Wv'], 'L1_attn_bv': _L1_attn_in['bv'], 'L1_attn_Wo': _L1_attn_in['Wo'], 'L1_attn_bo': _L1_attn_in['bo'], 'L1_ffn_Wg': _L1_ffn_in['Wg'], 'L1_ffn_W1': _L1_ffn_in['W1'], 'L1_ffn_b1': _L1_ffn_in['b1'], 'L1_ffn_W2': _L1_ffn_in['W2'], 'L1_ffn_b2': _L1_ffn_in['b2'], 'L1_ffn_Ws1': _L1_ffn_in['Ws1'], 'L1_ffn_bs1': _L1_ffn_in['bs1'], 'L1_ffn_Ws2': _L1_ffn_in['Ws2'], 'L1_ffn_bs2': _L1_ffn_in['bs2']}
    _x0 = _d['L0_attn_x']
    _d['L0_attn_x'] = jax.random.normal(jax.random.fold_in(jax.random.key(seed), 1), (2, 1024, 128), dtype=_x0.dtype)
    del _x0
    return _d

def reference(L0_attn_x, L0_attn_Wq, L0_attn_bq, L0_attn_Wk, L0_attn_bk, L0_attn_Wv, L0_attn_bv, L0_attn_Wo, L0_attn_bo, L0_ffn_Wr, L0_ffn_br, L0_ffn_W1, L0_ffn_b1, L0_ffn_W2, L0_ffn_b2, L1_attn_Wq, L1_attn_bq, L1_attn_Wk, L1_attn_bk, L1_attn_Wv, L1_attn_bv, L1_attn_Wo, L1_attn_bo, L1_ffn_Wg, L1_ffn_W1, L1_ffn_b1, L1_ffn_W2, L1_ffn_b2, L1_ffn_Ws1, L1_ffn_bs1, L1_ffn_Ws2, L1_ffn_bs2):

    def _L0_attn_ref(x, Wq, bq, Wk, bk, Wv, bv, Wo, bo):
        import jax, jax.numpy as jnp
        import numpy as np
        NEG = 10000.0
        q = jax.nn.relu(x @ Wq + bq)
        k = jax.nn.relu(x @ Wk + bk)
        v = jax.nn.relu(x @ Wv + bv)
        D = q.shape[-1]
        e = jnp.einsum('bqd,bkd->bqk', q, k) / jnp.sqrt(jnp.float32(D))
        S = e.shape[-1]
        causal = (jnp.arange(S)[None, :] > jnp.arange(S)[:, None]).astype(e.dtype)
        e = e - NEG * causal[None, :, :]
        e = jnp.exp(e - jnp.max(e, axis=-1, keepdims=True))
        attn = e / jnp.sum(e, axis=-1, keepdims=True)
        y = jnp.einsum('bqk,bkd->bqd', attn, v)
        return jax.nn.relu(y @ Wo + bo)

    def _L0_ffn_ref(x, Wr, br, W1, b1, W2, b2):
        import jax, jax.numpy as jnp
        import numpy as np
        D_MODEL, D_FF, N_EXP = (128, 512, 8)
        B, S, D = x.shape
        xf = x.reshape(-1, D)
        logits = xf @ Wr.T + br
        expert_idx = jnp.argmax(logits, axis=-1)
        h = jax.nn.relu(jnp.einsum('td,efd->etf', xf, W1) + b1[:, None, :])
        y = jnp.einsum('etf,edf->etd', h, W2) + b2[:, None, :]
        out = y[expert_idx, jnp.arange(xf.shape[0])]
        return out.reshape(B, S, D)

    def _L1_attn_ref(x, Wq, bq, Wk, bk, Wv, bv, Wo, bo):
        import jax, jax.numpy as jnp
        import numpy as np
        D_MODEL = 128
        N_HEADS = 16
        HEAD_DIM = D_MODEL // N_HEADS
        BATCH = 2
        SEQ = 256

        def _alibi_bias(seq_len, n_heads, dtype):
            slopes = 1.0 / 2.0 ** (jnp.arange(n_heads, dtype=dtype) / n_heads)
            rel = jnp.arange(seq_len, dtype=dtype)[None, :] - jnp.arange(seq_len, dtype=dtype)[:, None]
            return slopes[:, None, None] * rel[None, :, :]
        B, S, D = x.shape
        H, Hd = (N_HEADS, HEAD_DIM)
        scale = Hd ** (-0.5)
        Q = (x @ Wq + bq).reshape(B, S, H, Hd)
        K = (x @ Wk + bk).reshape(B, S, H, Hd)
        V = (x @ Wv + bv).reshape(B, S, H, Hd)
        scores = jnp.einsum('bqhd,bkhd->bhqk', Q, K) * scale
        scores = scores + _alibi_bias(S, H, x.dtype)[None]
        attn = jax.nn.softmax(scores, axis=-1)
        out = jnp.einsum('bhqk,bkhd->bqhd', attn, V).reshape(B, S, D)
        return out @ Wo + bo

    def _L1_ffn_ref(hidden_states, Wg, W1, b1, W2, b2, Ws1, bs1, Ws2, bs2):
        import jax, jax.numpy as jnp
        import numpy as np
        B, S, H = (2, 256, 128)
        F = 512
        E = 8
        TOP_K = 2
        SHARED_SCALE = 0.1
        EPS = 1e-09

        def _moe_forward(x3, Wg, W1, b1, W2, b2, Ws1, bs1, Ws2, bs2):
            b, s, h = x3.shape
            x = x3.reshape(-1, h)
            T = x.shape[0]
            logits = x @ Wg
            probs = jax.nn.softmax(logits, axis=-1)
            vals, idx = jax.lax.top_k(probs, TOP_K)
            weights = vals / (jnp.sum(vals, axis=-1, keepdims=True) + EPS)
            cw = jnp.zeros((T, E), dtype=x.dtype).at[jnp.arange(T)[:, None], idx].set(weights)
            hpre = jnp.einsum('th,ehf->tef', x, W1) + b1
            act = jax.nn.silu(hpre)
            y = jnp.einsum('tef,efh->teh', act, W2) + b2
            out = jnp.einsum('te,teh->th', cw, y)
            shared = jax.nn.silu(x @ Ws1 + bs1) @ Ws2 + bs2
            out = out + SHARED_SCALE * shared
            return out.reshape(b, s, h)
        return _moe_forward(hidden_states, Wg, W1, b1, W2, b2, Ws1, bs1, Ws2, bs2)
    x = L0_attn_x
    xn = _layernorm(x, axis=-1)
    s = _L0_attn_ref(xn, L0_attn_Wq, L0_attn_bq, L0_attn_Wk, L0_attn_bk, L0_attn_Wv, L0_attn_bv, L0_attn_Wo, L0_attn_bo)
    g = _silu(_L0_ffn_ref(xn, L0_ffn_Wr, L0_ffn_br, L0_ffn_W1, L0_ffn_b1, L0_ffn_W2, L0_ffn_b2))
    x = x + s * g
    xn = _layernorm(x, axis=-1)
    s = _L1_attn_ref(xn, L1_attn_Wq, L1_attn_bq, L1_attn_Wk, L1_attn_bk, L1_attn_Wv, L1_attn_bv, L1_attn_Wo, L1_attn_bo)
    g = _silu(_L1_ffn_ref(xn, L1_ffn_Wg, L1_ffn_W1, L1_ffn_b1, L1_ffn_W2, L1_ffn_b2, L1_ffn_Ws1, L1_ffn_bs1, L1_ffn_Ws2, L1_ffn_bs2))
    x = x + s * g
    return x

_drawn_inputs = setup_inputs


def setup_inputs(seed=0):
    import zlib

    import numpy as np

    out = dict(_drawn_inputs(seed))
    spreads = {'L0_attn_bq': (0.0, 0.8),
     'L0_attn_bk': (0.0, 0.8),
     'L0_attn_bv': (0.0, 0.8),
     'L0_attn_bo': (0.0, 0.8),
     'L1_attn_bq': (0.0, 0.8),
     'L1_attn_bk': (0.0, 2.0),
     'L1_attn_bv': (0.0, 0.8),
     'L1_attn_bo': (0.0, 0.8),
     'L1_ffn_b1': (0.0, 0.8),
     'L1_ffn_b2': (0.0, 0.8),
     'L1_ffn_bs1': (0.0, 0.8),
     'L1_ffn_bs2': (0.0, 2.0)}
    factors = {'L0_attn_Wq': 8.0,
     'L0_attn_Wk': 8.0,
     'L0_attn_Wv': 8.0,
     'L0_ffn_br': 5.078,
     'L0_ffn_b1': 8.0,
     'L0_ffn_b2': 8.0,
     'L1_attn_Wq': 8.0,
     'L1_attn_Wk': 8.0,
     'L1_attn_Wv': 8.0,
     'L1_attn_Wo': 8.0,
     'L1_ffn_Wg': 8.0,
     'L1_ffn_W1': 8.0,
     'L1_ffn_W2': 8.0,
     'L1_ffn_Ws1': 8.0,
     'L1_ffn_Ws2': 8.0}
    for name, (base, spread) in spreads.items():
        noise = np.random.default_rng([zlib.crc32(name.encode()), seed]).standard_normal(out[name].shape)
        drawn = base * np.exp(spread * noise) if base else spread * noise
        out[name] = jnp.asarray(drawn.astype(out[name].dtype))
    for name, factor in factors.items():
        out[name] = (out[name] * factor).astype(out[name].dtype)
    return out
```

```python
import numpy as np

import concourse.bass as bass
from concourse import mybir

FP32 = mybir.dt.float32
BF16 = mybir.dt.bfloat16
ALU = mybir.AluOpType
ACT = mybir.ActivationFunctionType
AX = mybir.AxisListType

P = 128
B, S, D = 2, 1024, 128
T = B * S
NT = T // P
TPB = S // P
BANK = 512
NC = T // BANK
F, E = 512, 8
FJ = F // P
H, HD = 16, 8
NEG = 10000.0
EPS = 1e-5
TOPK_EPS = 1e-9
SHARED = 0.1

PARTS = 3
PROD_ROWS = PARTS * PARTS * HD
ALIBI_ROWS = PARTS
MAX_ROW = 96
V_COLS = 32


class Lane:

    def __init__(self, nc, engine, name):
        self.e = engine
        self.sem = nc.alloc_semaphore(name)
        self.count = 0
        self.seen = {}

    def did(self, instruction):
        self.count += 1
        instruction.then_inc(self.sem, 1)
        return (self.sem, self.count)

    def wait(self, *ticks):
        for tick in ticks:
            if tick is None:
                continue
            sem, value = tick
            if self.seen.get(sem.name, 0) < value:
                self.e.wait_ge(sem, value)
                self.seen[sem.name] = value


class Loads:

    def __init__(self, nc, name):
        self.sem = nc.alloc_semaphore(name)
        self.count = 0

    def did(self, instruction):
        self.count += 16
        instruction.then_inc(self.sem, 16)
        return (self.sem, self.count)


class Slots:

    def __init__(self, buffers):
        self.buffers = buffers
        self.free = [()] * len(buffers)
        self.n = 0

    def take(self):
        i = self.n % len(self.buffers)
        self.n += 1
        return i, self.buffers[i], self.free[i]

    def release(self, i, *ticks):
        self.free[i] = ticks


def build(nc, a, out):
    pe = Lane(nc, nc.tensor, "pe_done")
    act = Lane(nc, nc.scalar, "act_done")
    dve = Lane(nc, nc.vector, "dve_done")
    pool = Lane(nc, nc.gpsimd, "pool_done")
    sp = Lane(nc, nc.sync, "sp_done")
    tensor, scalar, vector, gpsimd, sync = nc.tensor, nc.scalar, nc.vector, nc.gpsimd, nc.sync

    def sb(name, shape, dt=FP32):
        return nc.alloc_sbuf_tensor(name, shape, dt)

    x = sb("x", [P, NT, D])
    xn = sb("xn", [P, NT, D])
    xnT = sb("xnT", [P, T])
    attn = sb("attn", [P, NT, D])
    ffn = sb("ffn", [P, NT, D])
    ident = sb("ident", [P, P])
    ident_b = sb("ident_b", [P, P], BF16)
    stats = sb("stats", [P, NT, 6])
    mv = sb("mv", [P, NT, 2])
    std = sb("std", [P, NT])
    rstd = sb("rstd", [P, NT])
    eps = sb("eps", [P, 1])
    wqkvo = sb("wqkvo", [P, 4, D])
    bqk = sb("bqk", [P, 2])
    bvo = sb("bvo", [P, 2, D])
    router_w = sb("router_w", [P, E])
    router_b = sb("router_b", [P, E])
    logits = sb("logits", [P, NT, E])
    mix = sb("mix", [P, NT, E + 1])
    mixT = sb("mixT", [E + 1, T])
    rt1 = sb("rt1", [P, NT, E])
    rt2 = sb("rt2", [P, NT, E])
    rt3 = sb("rt3", [P, NT, E])
    rcol = sb("rcol", [P, NT])
    rcol2 = sb("rcol2", [P, NT])
    rcol3 = sb("rcol3", [P, NT])
    first_rank = sb("first_rank", [P, E])
    b1 = sb("b1", [P, E + 1, FJ])
    b2 = sb("b2", [E + 1, D])
    w_ring = [(sb(f"w1_{i}", [P, F]), sb(f"w2_{i}", [P, FJ, D])) for i in range(3)]
    hT = [sb(f"hT{i}", [P, FJ, BANK]) for i in range(2)]

    psum = nc.alloc_psum_tensor("psum", [P, 8 * BANK], FP32)
    pairs = Slots([psum[:, 2 * BANK:4 * BANK], psum[:, 4 * BANK:6 * BANK]])
    small = Slots([psum[:, 0:BANK], psum[:, BANK:2 * BANK]])
    accum = Slots([psum[:, 6 * BANK:7 * BANK], psum[:, 7 * BANK:8 * BANK]])

    ld_x = [Loads(nc, f"ld_x{c}") for c in range(NC)]
    ld_w = Loads(nc, "ld_w")
    ld_exp = [Loads(nc, f"ld_exp{i}") for i in range(3)]
    st_out = Loads(nc, "st_out")

    pool.did(gpsimd.memset(ident[:, :], 0.0))
    t = pool.did(gpsimd.memset(ident_b[:, :], 0.0))
    pool.wait(t)
    for m in (ident, ident_b):
        ident_done = pool.did(gpsimd.affine_select(
            out=m[:, :], in_=m[:, :], compare_op=ALU.not_equal, fill=1.0, base=0,
            pattern=[[-1, P]], channel_multiplier=1))
    for e in range(E):
        rank_done = pool.did(gpsimd.memset(first_rank[:, e:e + 1], float(E - e)))
    eps_done = pool.did(gpsimd.memset(eps[:, :], EPS))

    x_dram = a["L0_attn_x"].rearrange("b (t p) d -> p (b t) d", p=P)
    x_in = []
    for c in range(NC):
        x_in.append(ld_x[c].did(sync.dma_start(x[:, 4 * c:4 * c + 4, :], x_dram[:, 4 * c:4 * c + 4, :])))

    def load_layer_weights(L, *after):
        sp.wait(*after)
        for i, w in enumerate(("Wq", "Wk", "Wv", "Wo")):
            ld_w.did(sync.dma_start(wqkvo[:, i, :], a[f"L{L}_attn_{w}"]))
        for i, w in enumerate(("bq", "bk")):
            ld_w.did(sync.dma_start(bqk[:, i:i + 1], a[f"L{L}_attn_{w}"].rearrange("(p o) -> p o", o=1)))
        for i, w in enumerate(("bv", "bo")):
            ld_w.did(sync.dma_start(bvo[:, i, :], a[f"L{L}_attn_{w}"].partition_broadcast(P)))
        ld_w.did(sync.dma_start(router_w[:, :], a[f"L{L}_router"]))
        if L == 0:
            ld_w.did(sync.dma_start(router_b[:, :], a["L0_ffn_br"].partition_broadcast(P)))
        n = E + L
        ld_w.did(sync.dma_start(b1[:, 0:n, :], a[f"L{L}_b1"]))
        return ld_w.did(sync.dma_start(b2[0:n, :], a[f"L{L}_b2"]))

    expert_slots = Slots(w_ring)

    def load_expert(L, e):
        i, (w1, w2), free = expert_slots.take()
        sp.wait(*free)
        ld_exp[i].did(sync.dma_start(w1[:, :], a[f"L{L}_W1"][e]))
        t = ld_exp[i].did(sync.dma_start(w2[:, :, :], a[f"L{L}_W2"][e].rearrange("(j p) d -> p j d", p=P)))
        return i, w1, w2, t

    def layernorm(ready, free_xn, free_xnT):
        dve.wait(*free_xn)
        for t in range(NT):
            dve.wait(ready[t // 4])
            last = dve.did(vector.bn_stats(stats[:, t, :], x[:, t, :]))
        dve.wait(last)
        for t in range(NT):
            last = dve.did(vector.bn_aggr(mv[:, t, :], stats[:, t, :]))
        act.wait(last, eps_done)
        last = act.did(scalar.activation(std[:, :], mv[:, :, 1], ACT.Sqrt, bias=eps[:, 0:1]))
        dve.wait(last)
        last = dve.did(vector.reciprocal(rstd[:, :], std[:, :]))
        dve.wait(last)
        normed = []
        for t in range(NT):
            normed.append(dve.did(vector.tensor_scalar(
                xn[:, t, :], x[:, t, :], mv[:, t, 0:1], rstd[:, t:t + 1], ALU.subtract, ALU.mult)))
        pe.wait(ident_done)
        act.wait(*free_xnT)
        chunks = []
        for c in range(NC):
            i, bank, free = small.take()
            pe.wait(*free, normed[4 * c + 3])
            for k in range(4):
                last = tensor.transpose(bank[:, k * P:(k + 1) * P], xn[:, 4 * c + k, :], ident[:, :])
            last = pe.did(last)
            act.wait(last)
            last = act.did(scalar.activation(xnT[:, c * BANK:(c + 1) * BANK], bank, ACT.Copy))
            small.release(i, last)
            chunks.append(last)
        return normed, chunks

    def router_logits(L, xnT_ready, weights):
        i, bank, free = small.take()
        pe.wait(*free, weights, xnT_ready[-1])
        for t in range(NT):
            last = tensor.matmul(bank[:, t * E:(t + 1) * E], xnT[:, t * P:(t + 1) * P], router_w[:, :],
                                 start=True, stop=True)
        last = pe.did(last)
        dve.wait(last)
        flat = bank[:, 0:NT * E].rearrange("p (t e) -> p t e", e=E)
        if L == 0:
            dve.wait(weights)
            last = dve.did(vector.tensor_tensor(
                logits[:, :, :], flat, router_b[:, :].unsqueeze(1).to_broadcast([P, NT, E]), ALU.add))
        else:
            last = dve.did(vector.tensor_copy(logits[:, :, :], flat))
        small.release(i, last)
        return last

    def over_experts(col):
        return col[:, :].unsqueeze(2).to_broadcast([P, NT, E])

    def one_hot_of_max(values, onehot, top, work, ready):
        dve.wait(ready)
        last = dve.did(vector.tensor_reduce(top[:, :], values[:, :, :], AX.X, ALU.max))
        dve.wait(last)
        last = dve.did(vector.tensor_tensor(work[:, :, :], values[:, :, :], over_experts(top), ALU.is_equal))
        dve.wait(last, rank_done)
        last = dve.did(vector.tensor_tensor(
            work[:, :, :], work[:, :, :], first_rank[:, :].unsqueeze(1).to_broadcast([P, NT, E]), ALU.mult))
        dve.wait(last)
        last = dve.did(vector.tensor_reduce(rcol3[:, :], work[:, :, :], AX.X, ALU.max))
        dve.wait(last)
        return dve.did(vector.tensor_tensor(onehot, work[:, :, :], over_experts(rcol3), ALU.is_equal))

    def transpose_mix(n, ready, free_mixT):
        act.wait(*free_mixT)
        for c in range(NC):
            i, bank, free = small.take()
            pe.wait(*free, ready)
            for k in range(4):
                last = tensor.transpose(bank[0:n, k * P:(k + 1) * P], mix[:, 4 * c + k, 0:n], ident[:, :])
            last = pe.did(last)
            act.wait(last)
            last = act.did(scalar.activation(mixT[0:n, c * BANK:(c + 1) * BANK], bank[0:n, :], ACT.Copy))
            small.release(i, last)
        return last

    hT_slots = Slots(hT)

    def experts_ffn(L, func, mix_ready, mixT_ready, xnT_ready, weights, first):
        n = E + L
        for c in range(NC):
            i, bank, free = accum.take()
            pe.wait(*free, mixT_ready, weights)
            for k in range(4):
                t = 4 * c + k
                last = tensor.matmul(bank[:, k * D:(k + 1) * D], mixT[0:n, t * P:(t + 1) * P], b2[0:n, :],
                                     start=True, stop=True)
            last = pe.did(last)
            dve.wait(last)
            last = dve.did(vector.tensor_copy(ffn[:, 4 * c:4 * c + 4, :], bank.rearrange("p (k d) -> p k d", d=D)))
            accum.release(i, last)
        dve.wait(last)
        loaded = list(first)
        act.wait(weights)
        dve.wait(mix_ready)
        pe.wait(xnT_ready)
        steps = [(e, c) for e in range(n) for c in range(NC)]
        up = {}
        summed = [None] * NT

        def project_up(e, c):
            slot, w1, w2, w_ready = loaded[e]
            pe.wait(w_ready)
            hi, h, h_free = hT_slots.take()
            for half in range(FJ // 2):
                i, pair, free = pairs.take()
                pe.wait(*free)
                for jj in range(2):
                    j = 2 * half + jj
                    last = tensor.matmul(pair[:, jj * BANK:(jj + 1) * BANK], w1[:, j * P:(j + 1) * P],
                                         xnT[:, c * BANK:(c + 1) * BANK], start=True, stop=True)
                last = pe.did(last)
                act.wait(last, *h_free)
                for jj in range(2):
                    j = 2 * half + jj
                    last = act.did(scalar.activation(h[:, j, :], pair[:, jj * BANK:(jj + 1) * BANK], func,
                                                     bias=b1[:, e, j:j + 1]))
                pairs.release(i, last)
            up[e, c] = (hi, h, last)

        def project_down(e, c):
            slot, w1, w2, w_ready = loaded[e]
            hi, h, h_ready = up.pop((e, c))
            i, bank, free = accum.take()
            pe.wait(*free, h_ready)
            for k in range(4):
                for j in range(FJ):
                    last = tensor.matmul(bank[:, k * D:(k + 1) * D], h[:, j, k * P:(k + 1) * P], w2[:, j, :],
                                         start=(j == 0), stop=(j == FJ - 1))
            last = pe.did(last)
            hT_slots.release(hi, last)
            if c == NC - 1:
                expert_slots.release(slot, last)
                if len(loaded) < n:
                    loaded.append(load_expert(L, len(loaded)))
            dve.wait(last)
            for k in range(4):
                t = 4 * c + k
                dve.wait(summed[t])
                summed[t] = dve.did(vector.scalar_tensor_tensor(
                    out=ffn[:, t, :], in0=bank[:, k * D:(k + 1) * D], scalar=mix[:, t, e:e + 1],
                    in1=ffn[:, t, :], op0=ALU.mult, op1=ALU.add))
            accum.release(i, summed[4 * c + 3])

        project_up(*steps[0])
        for n_step in range(len(steps)):
            if n_step + 1 < len(steps):
                project_up(*steps[n_step + 1])
            project_down(*steps[n_step])
        return summed[NT - 1], pe.did_last

    def gate(attn_ready, ffn_ready, store):
        done = []
        act.wait(ffn_ready)
        silu = [act.did(scalar.activation(ffn[:, 4 * c:4 * c + 4, :], ffn[:, 4 * c:4 * c + 4, :], ACT.Silu))
                for c in range(NC)]
        dve.wait(attn_ready)
        for c in range(NC):
            part = slice(4 * c, 4 * c + 4)
            dve.wait(silu[c])
            last = dve.did(vector.tensor_tensor(ffn[:, part, :], ffn[:, part, :], attn[:, part, :], ALU.mult))
            dve.wait(last)
            last = dve.did(vector.tensor_tensor(x[:, part, :], x[:, part, :], ffn[:, part, :], ALU.add))
            done.append(last)
            if store:
                sp.wait(last)
                st_out.did(sync.dma_start(out.rearrange("b (t p) d -> p (b t) d", p=P)[:, part, :], x[:, part, :]))
        return done

    def project_features(w, bias, target, func, scale, xnT_ready, weights, free):
        pe.wait(xnT_ready, weights)
        act.wait(weights)
        act.wait(*free)
        done = []
        for c in range(NC):
            i, bank, bank_free = accum.take()
            pe.wait(*bank_free)
            last = pe.did(tensor.matmul(bank, wqkvo[:, w, :], xnT[:, c * BANK:(c + 1) * BANK], start=True, stop=True))
            act.wait(last)
            last = act.did(scalar.activation(target[:, c * BANK:(c + 1) * BANK], bank, func, bias=bias))
            accum.release(i, last)
            done.append(last)
        return done

    def value_products(xnT_ready, weights):
        pe.wait(xnT_ready, weights)
        for c in range(NC):
            i, bank, free = accum.take()
            pe.wait(*free)
            for k in range(4):
                t = 4 * c + k
                last = tensor.matmul(bank[:, k * D:(k + 1) * D], xnT[:, t * P:(t + 1) * P], wqkvo[:, 2, :],
                                     start=True, stop=True)
            yield c, i, bank.rearrange("p (k d) -> p k d", d=D), pe.did(last)

    def bias_of(i):
        return bvo[:, i, :].unsqueeze(1).to_broadcast([P, 4, D])

    weights = load_layer_weights(0)
    first = [load_expert(0, e) for e in range(3)]
    normed, xnT_chunks = layernorm(x_in, (), ())
    xnT_ready = xnT_chunks[-1]

    t = router_logits(0, xnT_chunks, weights)
    mix_ready = one_hot_of_max(logits, mix[:, :, 0:E], rcol, rt1, t)
    mixT_ready = transpose_mix(E, mix_ready, ())

    scope0 = [nc.sbuf_tensor(*s) for s in (
        ("qT", [P, T], FP32), ("kT", [P, T], FP32), ("v", [P, NT, D], FP32),
        ("causal", [P, S + (TPB - 1) * P], FP32), ("yT", [P, 2, P], FP32),
        ("scores", [P, 2, S], FP32), ("probs", [P, 2, S], FP32), ("probsT", [P, 2, S], FP32),
        ("l0_cols", [P, 4, NT], FP32))]
    qT, kT, v, causal, yT, scores, probs, probsT, l0_cols = [s.__enter__() for s in scope0]

    t = pool.did(gpsimd.memset(causal[:, :], 0.0))
    pool.wait(t)
    causal_done = pool.did(gpsimd.affine_select(
        out=causal[:, :], in_=causal[:, :], compare_op=ALU.is_ge, fill=-NEG, base=(TPB - 1) * P,
        pattern=[[-1, S + (TPB - 1) * P]], channel_multiplier=1))

    q_done = project_features(0, bqk[:, 0:1], qT, ACT.Relu, 1.0, xnT_ready, weights, ())
    k_done = project_features(1, bqk[:, 1:2], kT, ACT.Relu, 1.0, xnT_ready, weights, ())
    dve.wait(weights)
    for c, i, bank, t in value_products(xnT_ready, weights):
        dve.wait(t)
        part = slice(4 * c, 4 * c + 4)
        t = dve.did(vector.tensor_tensor(v[:, part, :], bank, bias_of(0), ALU.add))
        accum.release(i, t)
        pool.wait(t)
        v_done = pool.did(gpsimd.tensor_relu(v[:, part, :], v[:, part, :]))

    neg_max, row_sum, inv_sum = (l0_cols[:, n, :] for n in range(3))
    dve.wait(causal_done)
    pe.wait(v_done, q_done[-1], k_done[-1])
    scaled, exped, transposed, multiplied = {}, {}, {}, {}

    def l0_scores(t):
        b, i = divmod(t, TPB)
        s, pair, free = pairs.take()
        pe.wait(*free)
        for c in range(S // BANK):
            last = tensor.matmul(pair[:, c * BANK:(c + 1) * BANK], qT[:, t * P:(t + 1) * P],
                                 kT[:, b * S + c * BANK:b * S + (c + 1) * BANK], start=True, stop=True)
        last = pe.did(last)
        dve.wait(last, exped.get(t - 2))
        lo = (TPB - 1 - i) * P
        last = dve.did(vector.scalar_tensor_tensor(
            out=scores[:, t % 2, :], in0=pair, scalar=1.0 / float(np.sqrt(np.float32(D))), in1=causal[:, lo:lo + S],
            op0=ALU.mult, op1=ALU.add))
        pairs.release(s, last)
        dve.wait(last)
        scaled[t] = dve.did(vector.tensor_reduce(neg_max[:, t:t + 1], scores[:, t % 2, :], AX.X, ALU.max, negate=True))
        act.wait(scaled[t], transposed.get(t - 2))
        exped[t] = act.did(scalar.activation(probs[:, t % 2, :], scores[:, t % 2, :], ACT.Exp,
                                             bias=neg_max[:, t:t + 1], accum_out=row_sum[:, t:t + 1]))

    def l0_transposes(t):
        s, pair, free = pairs.take()
        pe.wait(*free, exped[t])
        for j in range(TPB):
            last = tensor.transpose(pair[:, j * P:(j + 1) * P], probs[:, t % 2, j * P:(j + 1) * P], ident[:, :])
        transposed[t] = pe.did(last)
        act.wait(transposed[t], multiplied.get(t - 2))
        copied = act.did(scalar.activation(probsT[:, t % 2, :], pair, ACT.Copy))
        pairs.release(s, copied)
        return copied

    yT_read = [None, None]

    def l0_output(t, copied):
        b, i = divmod(t, TPB)
        s, bank, free = small.take()
        pe.wait(*free, copied)
        for j in range(TPB):
            last = tensor.matmul(bank[:, 0:P], v[:, b * TPB + j, :], probsT[:, t % 2, j * P:(j + 1) * P],
                                 start=(j == 0), stop=(j == TPB - 1))
        multiplied[t] = pe.did(last)
        dve.wait(multiplied[t], yT_read[t % 2])
        copied = dve.did(vector.tensor_copy(yT[:, t % 2, :], bank[:, 0:P]))
        small.release(s, copied)
        s, bank, free = small.take()
        pe.wait(*free, copied)
        last = yT_read[t % 2] = pe.did(tensor.matmul(bank[:, 0:D], yT[:, t % 2, :], wqkvo[:, 3, :], start=True, stop=True))
        dve.wait(exped[t])
        r = dve.did(vector.reciprocal(inv_sum[:, t:t + 1], row_sum[:, t:t + 1]))
        dve.wait(last, r)
        last = dve.did(vector.scalar_tensor_tensor(
            out=attn[:, t, :], in0=bank[:, 0:D], scalar=inv_sum[:, t:t + 1], in1=bvo[:, 1, :],
            op0=ALU.mult, op1=ALU.add))
        small.release(s, last)
        pool.wait(last)
        return pool.did(gpsimd.tensor_relu(attn[:, t, :], attn[:, t, :]))

    l0_scores(0)
    for t in range(NT):
        if t + 1 < NT:
            l0_scores(t + 1)
        attn_ready = l0_output(t, l0_transposes(t))

    pe.did_last = None
    ffn_ready, _ = experts_ffn(0, ACT.Relu, mix_ready, mixT_ready, xnT_ready, weights, first)
    x_done = gate(attn_ready, ffn_ready, False)
    for s in reversed(scope0):
        s.__exit__(None, None, None)

    weights = load_layer_weights(1, x_done[-1])
    first = [load_expert(1, e) for e in range(3)]
    normed, xnT_chunks = layernorm(x_done, (), (x_done[-1],))
    xnT_ready = xnT_chunks[-1]

    last = router_logits(1, xnT_chunks, weights)
    dve.wait(last)
    last = dve.did(vector.tensor_reduce(rcol[:, :], logits[:, :, :], AX.X, ALU.max))
    dve.wait(last)
    last = dve.did(vector.tensor_tensor(logits[:, :, :], logits[:, :, :], over_experts(rcol), ALU.subtract))
    act.wait(last)
    last = act.did(scalar.activation(logits[:, :, :], logits[:, :, :], ACT.Exp))
    dve.wait(last)
    last = dve.did(vector.tensor_reduce(rcol[:, :], logits[:, :, :], AX.X, ALU.add))
    dve.wait(last)
    last = dve.did(vector.reciprocal(rcol[:, :], rcol[:, :]))
    dve.wait(last)
    last = dve.did(vector.tensor_tensor(logits[:, :, :], logits[:, :, :], over_experts(rcol), ALU.mult))
    last = one_hot_of_max(logits, rt2[:, :, :], rcol, rt1, last)
    dve.wait(last)
    last = dve.did(vector.scalar_tensor_tensor(out=rt3[:, :, :], in0=rt2[:, :, :], scalar=-2.0, in1=logits[:, :, :],
                                               op0=ALU.mult, op1=ALU.add))
    last = one_hot_of_max(rt3, rt1[:, :, :], rcol2, rt1, last)
    dve.wait(last)
    last = dve.did(vector.tensor_tensor(rt1[:, :, :], rt1[:, :, :], rt2[:, :, :], ALU.add))
    last2 = dve.did(vector.tensor_tensor(rcol3[:, :], rcol[:, :], rcol2[:, :], ALU.add))
    dve.wait(last, last2)
    last = dve.did(vector.tensor_tensor(rt1[:, :, :], rt1[:, :, :], logits[:, :, :], ALU.mult))
    last2 = dve.did(vector.tensor_scalar(rcol3[:, :], rcol3[:, :], TOPK_EPS, None, ALU.add))
    dve.wait(last2)
    last2 = dve.did(vector.reciprocal(rcol3[:, :], rcol3[:, :]))
    dve.wait(last, last2)
    dve.did(vector.memset(mix[:, :, E:E + 1], SHARED))
    mix_ready = dve.did(vector.tensor_tensor(mix[:, :, 0:E], rt1[:, :, :], over_experts(rcol3), ALU.mult))
    mixT_ready = transpose_mix(E + 1, mix_ready, (x_done[-1],))

    scope1 = [nc.sbuf_tensor(*s) for s in (
        ("proj", [P, T], FP32), ("rest", [P, T], FP32), ("part0", [P, T], BF16), ("part1", [P, T], BF16),
        ("part2", [P, T], BF16), ("v_aug", [P, NT, H, V_COLS], FP32), ("q_scale", [P, 1], FP32))]
    proj, rest, part0, part1, part2, v_aug, bq_scaled = [s.__enter__() for s in scope1]
    parts = (part0, part1, part2)
    RING = 4
    stacks = []
    for n in range(RING):
        s = [nc.sbuf_tensor(f"{w}_stack{n}", [P, S], BF16) for w in "qk"]
        scope1 += s
        stacks.append([h.__enter__() for h in s])
    more = [nc.sbuf_tensor(*s) for s in (
        ("exps", [P, 4, 2 * BANK], FP32), ("heads", [P, 2, BANK], FP32), ("merged", [P, 2, 4, D], FP32),
        ("mergedT", [P, 2, BANK], FP32), ("row_max", [P, 2, TPB], FP32), ("neg_row_max", [P, 2, TPB], BF16),
        ("neg_row_maxT", [TPB, 2, P], BF16), ("recips", [P, 2, 4, 4], FP32), ("heads_all", [P, 2, 4, BANK], FP32))]
    scope1 += more
    exps, heads, merged, mergedT, row_max, neg_row_max, neg_row_maxT, recips, heads_all = [s.__enter__() for s in more]
    split_dram = [nc.dram_tensor(f"split_{w}", [PARTS, P, T], BF16).ap() for w in "qk"]

    for q_stack, k_stack in stacks:
        for buf in (q_stack, k_stack):
            pool.did(gpsimd.memset(buf[:, :], 0.0))
    stack_const = (pool.sem, pool.count)
    const_sem = Loads(nc, "ld_const")
    sp.wait(stack_const)
    for q_stack, k_stack in stacks:
        const_sem.did(sync.dma_start(q_stack[PROD_ROWS:PROD_ROWS + ALIBI_ROWS, :], a["ones_rows"].bitcast(BF16)))
        consts_in = const_sem.did(sync.dma_start(k_stack[MAX_ROW:MAX_ROW + 1, :], a["ones_rows"][0:1, :].bitcast(BF16)))

    split_sem = [Loads(nc, f"st_split_{w}") for w in "qk"]
    dve.wait(weights)
    t = dve.did(vector.tensor_scalar(bq_scaled[:, :], bqk[:, 0:1], HD ** -0.5, None, ALU.mult))
    act.wait(t)
    split_done = []
    stored = ()
    for w, bias, scale in ((0, bq_scaled[:, 0:1], HD ** -0.5), (1, bqk[:, 1:2], 1.0)):
        act.wait(*stored)
        pe.wait(xnT_ready, weights)
        for c in range(NC):
            cols = slice(c * BANK, (c + 1) * BANK)
            i, bank, bank_free = accum.take()
            pe.wait(*bank_free)
            last = pe.did(tensor.matmul(bank, wqkvo[:, w, :], xnT[:, cols], start=True, stop=True))
            act.wait(last)
            last = act.did(scalar.activation(proj[:, cols], bank, ACT.Identity, bias=bias, scale=scale))
            accum.release(i, last)
            dve.wait(last, *stored)
            last = dve.did(vector.tensor_copy(parts[0][:, cols], proj[:, cols]))
            for n in (1, 2):
                src = proj if n == 1 else rest
                dve.wait(last)
                last = dve.did(vector.tensor_tensor(rest[:, cols], src[:, cols], parts[n - 1][:, cols], ALU.subtract))
                dve.wait(last)
                last = dve.did(vector.tensor_copy(parts[n][:, cols], rest[:, cols]))
        sp.wait(last)
        for n in range(PARTS):
            t = split_sem[w].did(sync.dma_start(split_dram[w][n], parts[n][:, :]))
        split_done.append(t)
        stored = (t,)

    t = pool.did(gpsimd.memset(v_aug[:, :, :, HD:V_COLS], 0.0))
    pool.wait(t)
    v_ones = pool.did(gpsimd.memset(v_aug[:, :, :, HD:HD + 1], 1.0))
    dve.wait(weights)
    for c, i, bank, t in value_products(xnT_ready, weights):
        dve.wait(t)
        for k in range(4):
            v_done = dve.did(vector.tensor_tensor(
                v_aug[:, 4 * c + k, :, 0:HD], bank[:, k, :].rearrange("p (h d) -> p h d", d=HD),
                bvo[:, 0, :].rearrange("p (h d) -> p h d", d=HD), ALU.add))
        accum.release(i, v_done)

    units = [(b, h) for b in range(B) for h in range(H)]
    stack_sem = [Loads(nc, f"ld_stack{n}") for n in range(RING)]
    max_sem = [Loads(nc, f"ld_max{n}") for n in range(RING)]
    stack_free = [() for _ in range(RING)]
    stack_in, max_in = {}, {}
    maxed = {}
    exp_slots = Slots([exps[:, n, :] for n in range(4)])
    sp.wait(*split_done)
    pe.wait(consts_in)

    def load_stack(u):
        b, h = units[u]
        n = u % RING
        q_stack, k_stack = stacks[n]
        sp.wait(*stack_free[n])
        for i in range(PARTS):
            q_src = split_dram[0][i, h * HD:(h + 1) * HD, b * S:(b + 1) * S]
            k_src = split_dram[1][:, h * HD:(h + 1) * HD, b * S:(b + 1) * S]
            rows = PARTS * HD
            stack_sem[n].did(sync.dma_start(
                q_stack[i * rows:(i + 1) * rows, :], q_src.unsqueeze(0).to_broadcast([PARTS, HD, S])))
            stack_sem[n].did(sync.dma_start(k_stack[i * rows:(i + 1) * rows, :], k_src))
        stack_in[u] = stack_sem[n].did(sync.dma_start(
            k_stack[PROD_ROWS:PROD_ROWS + ALIBI_ROWS, :], a["alibi"][h].bitcast(BF16)))

    def find_max(u):
        b, h = units[u]
        n, r = u % RING, u % 2
        q_stack, k_stack = stacks[n]
        pe.wait(stack_in[u])
        for i in range(TPB):
            s, pair, free = pairs.take()
            pe.wait(*free)
            for c in range(S // BANK):
                last = tensor.matmul(pair[:, c * BANK:(c + 1) * BANK], q_stack[0:MAX_ROW, i * P:(i + 1) * P],
                                     k_stack[0:MAX_ROW, c * BANK:(c + 1) * BANK], start=True, stop=True)
            last = pe.did(last)
            dve.wait(last)
            last = dve.did(vector.tensor_reduce(row_max[:, r, i:i + 1], pair, AX.X, ALU.max))
            pairs.release(s, last)
        dve.wait(last, maxed.get(u - 2))
        last = dve.did(vector.tensor_scalar(neg_row_max[:, r, :], row_max[:, r, :], -1.0, None, ALU.mult))
        maxed[u] = last

    def place_max(u):
        n, r = u % RING, u % 2
        q_stack = stacks[n][0]
        s, bank, free = small.take()
        pe.wait(*free, maxed[u])
        flipped = bank.bitcast(BF16)[0:TPB, 0:P]
        last = maxed[u] = pe.did(tensor.transpose(flipped, neg_row_max[:, r, :], ident_b[:, :]))
        dve.wait(last, max_in.get(u - 2))
        last = dve.did(vector.tensor_copy(neg_row_maxT[:, r, :], flipped))
        small.release(s, last)
        sp.wait(last)
        max_in[u] = max_sem[n].did(sync.dma_start(
            q_stack[MAX_ROW:MAX_ROW + 1, :], neg_row_maxT[:, r, :]))

    out_bank = {}

    def attend(u):
        b, h = units[u]
        n = u % RING
        q_stack, k_stack = stacks[n]
        quarter = h % 4
        for qc in range(S // BANK):
            if quarter == 0:
                out_bank[qc] = accum.take()
            slot, bank, bank_free = out_bank[qc]
            if quarter == 0:
                pe.wait(*bank_free)
            q_cols = slice(qc * BANK, (qc + 1) * BANK)
            ready = []

            def multiply(jj):
                s, p_buf, t = ready[jj]
                pe.wait(t)
                for m in range(2):
                    j = 2 * jj + m
                    last = tensor.matmul(bank[quarter * V_COLS:(quarter + 1) * V_COLS, :],
                                         v_aug[:, b * TPB + j, h, :], p_buf[:, m * BANK:(m + 1) * BANK],
                                         start=(j == 0), stop=(j == TPB - 1), tile_position=(0, quarter * V_COLS))
                last = pe.did(last)
                exp_slots.release(s, last)
                return last

            for jj in range(TPB // 2):
                s, pair, free = pairs.take()
                pe.wait(*free, max_in[u])
                for m in range(2):
                    j = 2 * jj + m
                    last = tensor.matmul(pair[:, m * BANK:(m + 1) * BANK], k_stack[0:MAX_ROW + 1, j * P:(j + 1) * P],
                                         q_stack[0:MAX_ROW + 1, q_cols], start=True, stop=True)
                last = pe.did(last)
                es, p_buf, p_free = exp_slots.take()
                act.wait(last, *p_free)
                t = act.did(scalar.activation(p_buf, pair, ACT.Exp))
                pairs.release(s, t)
                ready.append((es, p_buf, t))
                if jj:
                    multiply(jj - 1)
            last = multiply(TPB // 2 - 1)
            if quarter == 3:
                dve.wait(last, heads_read[qc])
                t = dve.did(vector.tensor_copy(heads_all[:, qc, h // 4, :], bank))
                accum.release(slot, t)
                heads_in[qc] = t
        stack_free[n] = (last,)

    heads_read, heads_in = [None, None], [None, None]
    merged_read, mergedT_read = [None, None], [None, None]
    pe.wait(v_ones, v_done)

    def merge(b, qc):
        for g in range(H // 4):
            s, bank, free = small.take()
            pe.wait(*free, heads_in[qc])
            for k in range(4):
                last = tensor.transpose(bank[:, k * P:(k + 1) * P], heads_all[:, qc, g, k * P:(k + 1) * P], ident[:, :])
            last = heads_read[qc] = pe.did(last)
            by_head = bank.rearrange("p (k h c) -> p k h c", k=4, c=V_COLS)
            dve.wait(last)
            last = dve.did(vector.reciprocal(recips[:, g % 2, :, :], by_head[:, :, :, HD]))
            dve.wait(last, merged_read[qc])
            last = dve.did(vector.tensor_tensor(
                merged[:, qc, :, g * 4 * HD:(g + 1) * 4 * HD].rearrange("p k (h d) -> p k h d", d=HD),
                by_head[:, :, :, 0:HD], recips[:, g % 2, :, :].unsqueeze(3).to_broadcast([P, 4, 4, HD]), ALU.mult))
            small.release(s, last)
        s, bank, free = small.take()
        pe.wait(*free, last)
        for k in range(4):
            last = tensor.transpose(bank[:, k * P:(k + 1) * P], merged[:, qc, k, :], ident[:, :])
        last = merged_read[qc] = pe.did(last)
        act.wait(last, mergedT_read[qc])
        last = act.did(scalar.activation(mergedT[:, qc, :], bank, ACT.Copy))
        small.release(s, last)
        s, bank, free = small.take()
        pe.wait(*free, last)
        for k in range(4):
            last = tensor.matmul(bank[:, k * D:(k + 1) * D], mergedT[:, qc, k * P:(k + 1) * P], wqkvo[:, 3, :],
                                 start=True, stop=True)
        last = mergedT_read[qc] = pe.did(last)
        dve.wait(last)
        t0 = b * TPB + 4 * qc
        last = dve.did(vector.tensor_tensor(attn[:, t0:t0 + 4, :], bank.rearrange("p (k d) -> p k d", d=D), bias_of(1), ALU.add))
        small.release(s, last)
        return last

    load_stack(0)
    load_stack(1)
    find_max(0)
    place_max(0)
    for u in range(len(units)):
        if u + 2 < len(units):
            load_stack(u + 2)
        if u + 1 < len(units):
            find_max(u + 1)
            place_max(u + 1)
        attend(u)
        if units[u][1] == H - 1:
            for qc in range(S // BANK):
                attn_ready = merge(units[u][0], qc)

    ffn_ready, _ = experts_ffn(1, ACT.Silu, mix_ready, mixT_ready, xnT_ready, weights, first)
    gate(attn_ready, ffn_ready, True)
    sync.wait_ge(st_out.sem, st_out.count)
    for s in reversed(scope1):
        s.__exit__(None, None, None)


def split_constant(values):
    parts, rest = [], values.astype(np.float32)
    for _ in range(PARTS):
        part = (rest.view(np.uint32) & np.uint32(0xFFFF0000)).view(np.float32)
        parts.append((part.view(np.uint32) >> 16).astype(np.uint16))
        rest = rest - part
    return np.stack(parts)


def kernel(**inputs):
    import concourse.bacc as bacc
    from concourse.bass_utils import run_bass_kernel_spmd

    g = {k: np.asarray(v) for k, v in inputs.items()}
    arrays = {k: g[k] for k in g if "_attn_" in k}
    arrays["L0_ffn_br"] = g["L0_ffn_br"]
    arrays["L0_router"] = g["L0_ffn_Wr"].T
    arrays["L0_W1"] = g["L0_ffn_W1"].transpose(0, 2, 1)
    arrays["L0_W2"] = g["L0_ffn_W2"].transpose(0, 2, 1)
    arrays["L0_b1"], arrays["L0_b2"] = g["L0_ffn_b1"], g["L0_ffn_b2"]
    arrays["L1_router"] = g["L1_ffn_Wg"]
    for w in ("W1", "W2", "b1", "b2"):
        arrays[f"L1_{w}"] = np.concatenate([g[f"L1_ffn_{w}"], g[f"L1_ffn_{w[0]}s{w[1]}"][None]])
    for L in range(2):
        arrays[f"L{L}_b1"] = arrays[f"L{L}_b1"].reshape(E + L, FJ, P).transpose(2, 0, 1)
    slopes = 1.0 / 2.0 ** (np.arange(H, dtype=np.float32) / H)
    rel = slopes[:, None].astype(np.float32) * (np.arange(S, dtype=np.float32) - (S - 1))[None, :]
    arrays["alibi"] = np.ascontiguousarray(split_constant(rel).transpose(1, 0, 2))
    arrays["ones_rows"] = split_constant(np.ones((ALIBI_ROWS, S)))[0]
    arrays = {k: np.ascontiguousarray(v) for k, v in arrays.items()}

    nc = bacc.Bacc("TRN2", target_bir_lowering=False, num_devices=1)
    aps = {k: nc.dram_tensor(k, v.shape, mybir.dt.from_np(v.dtype), kind="ExternalInput").ap() for k, v in arrays.items()}
    out = nc.dram_tensor("y", (B, S, D), FP32, kind="ExternalOutput").ap()
    build(nc, aps, out)
    r = run_bass_kernel_spmd(nc, [arrays], core_ids=[0])
    return r.results[0]["y"]
```

```python
import numpy as np

import concourse.bass as bass
from concourse import mybir

FP32 = mybir.dt.float32
BF16 = mybir.dt.bfloat16
ALU = mybir.AluOpType
ACT = mybir.ActivationFunctionType
AX = mybir.AxisListType

P = 128
B, S, D = 2, 1024, 128
T = B * S
NT = T // P
TPB = S // P
BANK = 512
NC = T // BANK
F, E = 512, 8
FJ = F // P
H, HD = 16, 8
NEG = 10000.0
EPS = 1e-5
TOPK_EPS = 1e-9
SHARED = 0.1

PARTS = 3
PROD_ROWS = PARTS * PARTS * HD
ALIBI_ROWS = PARTS
MAX_ROW = 96
V_COLS = 32


class Lane:

    def __init__(self, nc, engine, name):
        self.nc, self.e, self.name = nc, engine, name
        self.restart("")

    def restart(self, where):
        self.sem = self.nc.alloc_semaphore(self.name + where)
        self.count = 0
        self.seen = {}

    def did(self, instruction):
        self.count += 1
        instruction.then_inc(self.sem, 1)
        return (self.sem, self.count)

    def wait(self, *ticks):
        for tick in ticks:
            if tick is None:
                continue
            sem, value = tick
            if self.seen.get(sem.name, 0) < value:
                self.e.wait_ge(sem, value)
                self.seen[sem.name] = value


class Loads:

    def __init__(self, nc, name):
        self.sem = nc.alloc_semaphore(name)
        self.count = 0

    def did(self, instruction):
        self.count += 16
        instruction.then_inc(self.sem, 16)
        return (self.sem, self.count)


class Slots:

    def __init__(self, buffers):
        self.buffers = buffers
        self.free = [()] * len(buffers)
        self.n = 0

    def take(self):
        i = self.n % len(self.buffers)
        self.n += 1
        return i, self.buffers[i], self.free[i]

    def release(self, i, *ticks):
        self.free[i] = ticks

    def all_free(self):
        self.free = [()] * len(self.buffers)
        self.n = 0


UNDERFLOW = 105.0


def slope(h):
    return 1.0 / 2.0 ** (h / H)


def near_tiles(h):
    return 2 if slope(h) * 2 * P - UNDERFLOW > 68 else 3


def blocks_of(L):
    return (L + 1) * NT + E - 1


MAX_BLOCKS = 48
GROUP = BANK // P
ARENA = 8192


def build(nc, a, out):
    pe = Lane(nc, nc.tensor, "pe_done")
    act = Lane(nc, nc.scalar, "act_done")
    dve = Lane(nc, nc.vector, "dve_done")
    pool = Lane(nc, nc.gpsimd, "pool_done")
    sp = Lane(nc, nc.sync, "sp_done")
    tensor, scalar, vector, gpsimd, sync = nc.tensor, nc.scalar, nc.vector, nc.gpsimd, nc.sync

    def sb(name, shape, dt=FP32):
        return nc.alloc_sbuf_tensor(name, shape, dt)

    x = sb("x", [P, NT, D])
    xn = sb("xn", [P, NT, D])
    xnT = sb("xnT", [P, T])
    attn = sb("attn", [P, NT, D])
    ffn = sb("ffn", [P, NT, D])
    ident = sb("ident", [P, P])
    ident_b = sb("ident_b", [P, P], BF16)
    stats = sb("stats", [P, NT, 6])
    mv = sb("mv", [P, NT, 2])
    std = sb("std", [P, NT])
    rstd = sb("rstd", [P, NT])
    eps = sb("eps", [P, 1])
    wqkvo = sb("wqkvo", [P, 4, D])
    bqk = sb("bqk", [P, 2])
    bvo = sb("bvo", [P, 2, D])
    router_w = sb("router_w", [P, E])
    router_b = sb("router_b", [P, E])
    logits = sb("logits", [P, NT, E])
    mix = sb("mix", [P, NT, E + 1])
    mixT = sb("mixT", [E + 1, T])
    rt1 = sb("rt1", [P, NT, E])
    rt2 = sb("rt2", [P, NT, E])
    rt3 = sb("rt3", [P, NT, E])
    rcol = sb("rcol", [P, NT])
    rcol2 = sb("rcol2", [P, NT])
    rcol3 = sb("rcol3", [P, NT])
    weight1 = sb("weight1", [P, NT])
    weight2 = sb("weight2", [P, NT])
    first_rank = sb("first_rank", [P, E])
    b1 = sb("b1", [P, E + 1, FJ])
    b2 = sb("b2", [E + 1, D])
    w1_all = sb("w1_all", [P, E, F])
    w1_block = sb("w1_block", [P, 2, F])
    w2_all = sb("w2_all", [P, E, FJ, D])
    shared_w1 = sb("shared_w1", [P, F])
    shared_w2 = sb("shared_w2", [P, FJ, D])
    ones_f = sb("ones_f", [P, NT * E])
    ones_b = sb("ones_b", [P, P], BF16)
    before = sb("before", [P, P], BF16)
    ids = sb("numbers", [P, 2, MAX_BLOCKS])
    chosen = sb("chosen", [P, E, NT], BF16)
    in_tile = sb("in_tile", [P, E, NT])
    upto = sb("upto", [P, E, NT])
    place = sb("place", [P, E, NT])
    by_expert = sb("by_expert", [P, 6, E + 1])
    over = sb("over", [P, E, NT])
    product = sb("product", [P, E, NT])
    slot_f = sb("slot_f", [P, NT])
    slots_u = [sb(f"slots{i}", [P, NT], mybir.dt.uint32) for i in range(2)]
    past = sb("past", [1, MAX_BLOCKS, E])
    block_f = sb("block_f", [1, MAX_BLOCKS])
    block_expert = [sb(f"block_expert{L}", [1, MAX_BLOCKS], mybir.dt.int32) for L in range(2)]
    zeros = sb("zeros", [P, 4 * D])
    routed_x = [nc.dram_tensor(f"routed_x{L}", [blocks_of(L) * P, D], FP32).ap() for L in range(2)]
    routed_y = [nc.dram_tensor(f"routed_y{L}", [blocks_of(L) * P, D], FP32).ap() for L in range(2)]

    psum = nc.alloc_psum_tensor("psum", [P, 8 * BANK], FP32)
    pairs = Slots([psum[:, 2 * BANK:4 * BANK], psum[:, 4 * BANK:6 * BANK]])
    small = Slots([psum[:, 0:BANK], psum[:, BANK:2 * BANK]])
    accum = Slots([psum[:, 6 * BANK:7 * BANK], psum[:, 7 * BANK:8 * BANK]])

    def rejoin(where, barrier=True):
        if barrier:
            nc.all_engine_barrier()
        for lane in (pe, act, dve, pool, sp):
            lane.restart(where)
        for slots in (pairs, small, accum):
            slots.all_free()

    ld_x = [Loads(nc, f"ld_x{c}") for c in range(NC)]
    ld_w = Loads(nc, "ld_w")
    ld_routed = [Loads(nc, f"ld_routed{L}") for L in range(2)]
    ld_shared = Loads(nc, "ld_shared")
    st_zero = Loads(nc, "st_zero")
    st_out = Loads(nc, "st_out")

    pool.did(gpsimd.memset(ident[:, :], 0.0))
    t = pool.did(gpsimd.memset(ident_b[:, :], 0.0))
    pool.wait(t)
    for m in (ident, ident_b):
        ident_done = pool.did(gpsimd.affine_select(
            out=m[:, :], in_=m[:, :], compare_op=ALU.not_equal, fill=1.0, base=0,
            pattern=[[-1, P]], channel_multiplier=1))
    for e in range(E):
        rank_done = pool.did(gpsimd.memset(first_rank[:, e:e + 1], float(E - e)))
    eps_done = pool.did(gpsimd.memset(eps[:, :], EPS))
    zeros_done = pool.did(gpsimd.memset(zeros[:, :], 0.0))
    pool.did(gpsimd.memset(ones_f[:, :], 1.0))
    pool.did(gpsimd.memset(ones_b[:, :], 1.0))
    t = pool.did(gpsimd.memset(before[:, :], 1.0))
    pool.wait(t)
    counting_done = pool.did(gpsimd.affine_select(
        out=before[:, :], in_=before[:, :], compare_op=ALU.is_gt, fill=0.0, base=0,
        pattern=[[1, P]], channel_multiplier=-1))

    ids_in = Loads(nc, "ld_ids").did(sync.dma_start(ids[:, :, :], a["ids"]))
    x_dram = a["L0_attn_x"].rearrange("b (t p) d -> p (b t) d", p=P)
    x_in = []
    for c in range(NC):
        x_in.append(ld_x[c].did(sync.dma_start(x[:, 4 * c:4 * c + 4, :], x_dram[:, 4 * c:4 * c + 4, :])))

    def load_layer_weights(L, *after):
        sp.wait(*after)
        for i, w in enumerate(("Wq", "Wk", "Wv", "Wo")):
            ld_w.did(sync.dma_start(wqkvo[:, i, :], a[f"L{L}_attn_{w}"]))
        for i, w in enumerate(("bq", "bk")):
            ld_w.did(sync.dma_start(bqk[:, i:i + 1], a[f"L{L}_attn_{w}"].rearrange("(p o) -> p o", o=1)))
        for i, w in enumerate(("bv", "bo")):
            ld_w.did(sync.dma_start(bvo[:, i, :], a[f"L{L}_attn_{w}"].partition_broadcast(P)))
        ld_w.did(sync.dma_start(router_w[:, :], a[f"L{L}_router"]))
        if L == 0:
            ld_w.did(sync.dma_start(router_b[:, :], a["L0_ffn_br"].partition_broadcast(P)))
        n = E + L
        ld_w.did(sync.dma_start(b1[:, 0:n, :], a[f"L{L}_b1"]))
        return ld_w.did(sync.dma_start(b2[0:n, :], a[f"L{L}_b2"]))

    def zero_routed(L):
        sp.wait(zeros_done)
        n = blocks_of(L)
        for g in range(0, n, GROUP):
            m = min(GROUP, n - g)
            t = st_zero.did(sync.dma_start(
                routed_x[L][g * P:(g + m) * P, :].rearrange("(k p) d -> p k d", p=P),
                zeros[:, 0:m * D].rearrange("p (k d) -> p k d", d=D)))
        return t

    def load_routed(L, after):
        sp.wait(*after)
        ld_routed[L].did(sync.dma_start(w1_all[:, :, :], a[f"L{L}_W1"][0:E].rearrange("e d f -> d e f")))
        return ld_routed[L].did(sync.dma_start(w2_all[:, :, :, :].rearrange("p e j d -> p (e j) d"),
                                               a[f"L{L}_W2"][0:E].rearrange("e (j p) d -> p (e j) d", p=P)))

    def layernorm(ready, free_xn, free_xnT):
        dve.wait(*free_xn)
        for t in range(NT):
            dve.wait(ready[t // 4])
            last = dve.did(vector.bn_stats(stats[:, t, :], x[:, t, :]))
        dve.wait(last)
        for t in range(NT):
            last = dve.did(vector.bn_aggr(mv[:, t, :], stats[:, t, :]))
        act.wait(last, eps_done)
        last = act.did(scalar.activation(std[:, :], mv[:, :, 1], ACT.Sqrt, bias=eps[:, 0:1]))
        dve.wait(last)
        last = dve.did(vector.reciprocal(rstd[:, :], std[:, :]))
        dve.wait(last)
        normed = []
        for t in range(NT):
            normed.append(dve.did(vector.tensor_scalar(
                xn[:, t, :], x[:, t, :], mv[:, t, 0:1], rstd[:, t:t + 1], ALU.subtract, ALU.mult)))
        pe.wait(ident_done)
        act.wait(*free_xnT)
        chunks = []
        for c in range(NC):
            i, bank, free = small.take()
            pe.wait(*free, normed[4 * c + 3])
            for k in range(4):
                last = tensor.transpose(bank[:, k * P:(k + 1) * P], xn[:, 4 * c + k, :], ident[:, :])
            last = pe.did(last)
            act.wait(last)
            last = act.did(scalar.activation(xnT[:, c * BANK:(c + 1) * BANK], bank, ACT.Copy))
            small.release(i, last)
            chunks.append(last)
        return normed, chunks

    def router_logits(L, xnT_ready, weights):
        i, bank, free = small.take()
        pe.wait(*free, weights, xnT_ready[-1])
        for t in range(NT):
            last = tensor.matmul(bank[:, t * E:(t + 1) * E], xnT[:, t * P:(t + 1) * P], router_w[:, :],
                                 start=True, stop=True)
        last = pe.did(last)
        dve.wait(last)
        flat = bank[:, 0:NT * E].rearrange("p (t e) -> p t e", e=E)
        if L == 0:
            dve.wait(weights)
            last = dve.did(vector.tensor_tensor(
                logits[:, :, :], flat, router_b[:, :].unsqueeze(1).to_broadcast([P, NT, E]), ALU.add))
        else:
            last = dve.did(vector.tensor_copy(logits[:, :, :], flat))
        small.release(i, last)
        return last

    def over_experts(col):
        return col[:, :].unsqueeze(2).to_broadcast([P, NT, E])

    def one_hot_of_max(values, onehot, top, work, ready):
        dve.wait(ready)
        last = dve.did(vector.tensor_reduce(top[:, :], values[:, :, :], AX.X, ALU.max))
        dve.wait(last)
        last = dve.did(vector.tensor_tensor(work[:, :, :], values[:, :, :], over_experts(top), ALU.is_equal))
        dve.wait(last, rank_done)
        last = dve.did(vector.tensor_tensor(
            work[:, :, :], work[:, :, :], first_rank[:, :].unsqueeze(1).to_broadcast([P, NT, E]), ALU.mult))
        dve.wait(last)
        last = dve.did(vector.tensor_reduce(rcol3[:, :], work[:, :, :], AX.X, ALU.max))
        dve.wait(last)
        return dve.did(vector.tensor_tensor(onehot, work[:, :, :], over_experts(rcol3), ALU.is_equal))

    def transpose_mix(n, ready, free_mixT):
        act.wait(*free_mixT)
        for c in range(NC):
            i, bank, free = small.take()
            pe.wait(*free, ready)
            for k in range(4):
                last = tensor.transpose(bank[0:n, k * P:(k + 1) * P], mix[:, 4 * c + k, 0:n], ident[:, :])
            last = pe.did(last)
            act.wait(last)
            last = act.did(scalar.activation(mixT[0:n, c * BANK:(c + 1) * BANK], bank[0:n, :], ACT.Copy))
            small.release(i, last)
        return last

    def dispatch(L, onehots, ready):
        n_blocks = blocks_of(L)
        by = "p e t -> p t e"
        as_et = [o.rearrange("p t e -> p e t") for o in onehots]
        dve.wait(ready, counting_done, ids_in)
        if L == 0:
            last = dve.did(vector.tensor_copy(chosen[:, :, :], as_et[0]))
        else:
            last = dve.did(vector.tensor_tensor(chosen[:, :, :], as_et[0], as_et[1], ALU.add))
        i, bank, free = small.take()
        pe.wait(*free, last)
        n = E * NT
        flat = chosen[:, :, :].rearrange("p e t -> p (e t)")
        tensor.matmul(bank[:, 0:n], before[:, :], flat, start=True, stop=True)
        last = pe.did(tensor.matmul(bank[:, n:2 * n], ones_b[:, :], flat, start=True, stop=True))
        rank = bank[:, 0:n].rearrange("p (e t) -> p e t", t=NT)
        dve.wait(last)
        last = dve.did(vector.tensor_copy(in_tile[:, :, :], bank[:, n:2 * n].rearrange("p (e t) -> p e t", t=NT)))
        dve.wait(last)
        last = dve.did(vector.tensor_tensor_scan(
            upto[:, :, :].rearrange("p e t -> p (e t)"), ones_f[:, :],
            in_tile[:, :, :].rearrange("p e t -> p (e t)"), 0.0, ALU.mult, ALU.add))
        cum, count, n_blk, end, base = (by_expert[:, m, :] for m in range(5))
        t = dve.did(vector.memset(by_expert[:, :, 0:1], 0.0))
        dve.wait(last, t)
        last = dve.did(vector.tensor_copy(cum[:, 1:E + 1], upto[:, :, NT - 1]))
        dve.wait(last)
        last = dve.did(vector.tensor_tensor(count[:, 1:E + 1], cum[:, 1:E + 1], cum[:, 0:E], ALU.subtract))
        dve.wait(last)
        last = dve.did(vector.tensor_tensor(
            over[:, :, :], count[:, 1:E + 1].unsqueeze(2).to_broadcast([P, E, NT]),
            ids[:, 1, 0:NT].unsqueeze(1).to_broadcast([P, E, NT]), ALU.is_gt))
        dve.wait(last)
        last = dve.did(vector.tensor_reduce(n_blk[:, 1:E + 1], over[:, :, :], AX.X, ALU.add))
        dve.wait(last)
        last = dve.did(vector.tensor_tensor_scan(end[:, 1:E + 1], ones_f[:, 0:E], n_blk[:, 1:E + 1], 0.0, ALU.mult, ALU.add))
        dve.wait(last)
        last = dve.did(vector.scalar_tensor_tensor(out=base[:, 0:E], in0=end[:, 0:E], scalar=float(P), in1=cum[:, 0:E],
                                                   op0=ALU.mult, op1=ALU.subtract))
        t = dve.did(vector.tensor_tensor(place[:, :, :], upto[:, :, :], in_tile[:, :, :], ALU.subtract))
        dve.wait(t)
        t = dve.did(vector.tensor_tensor(place[:, :, :], rank, place[:, :, :], ALU.add))
        small.release(i, t)
        dve.wait(t, last)
        last = dve.did(vector.tensor_tensor(
            place[:, :, :], place[:, :, :], base[:, 0:E].unsqueeze(2).to_broadcast([P, E, NT]), ALU.add))
        for k, o in enumerate(as_et):
            dve.wait(last)
            last = dve.did(vector.tensor_tensor(product[:, :, :], place[:, :, :], o, ALU.mult))
            dve.wait(last)
            last = dve.did(vector.tensor_reduce(slot_f[:, :], product[:, :, :].rearrange(by), AX.X, ALU.add))
            dve.wait(last)
            placed = last = dve.did(vector.tensor_copy(slots_u[k][:, :], slot_f[:, :]))
        last = dve.did(vector.tensor_tensor(
            past[:, 0:n_blocks, :], end[0:1, 1:E + 1].unsqueeze(1).to_broadcast([1, n_blocks, E]),
            ids[0:1, 0, 0:n_blocks].unsqueeze(2).to_broadcast([1, n_blocks, E]), ALU.is_le))
        dve.wait(last)
        last = dve.did(vector.tensor_reduce(block_f[:, 0:n_blocks], past[:, 0:n_blocks, :], AX.X, ALU.add))
        dve.wait(last)
        named = dve.did(vector.tensor_scalar(block_expert[L][:, 0:n_blocks], block_f[:, 0:n_blocks], float(E - 1), None, ALU.min))
        return placed, named

    st_rows = [Loads(nc, f"st_rows{L}") for L in range(2)]

    def scatter_rows(L, placed, normed, zeroed):
        pool.wait(placed, normed, zeroed)
        for k in range(L + 1):
            for t in range(NT):
                last = st_rows[L].did(gpsimd.indirect_dma_start(
                    out=routed_x[L][:, :], out_offset=bass.IndirectOffsetOnAxis(ap=slots_u[k][:, t:t + 1], axis=0),
                    in_=xn[:, t, :], in_offset=None))
        return last

    def routed_ffn(L, func, bufs, named, scattered, routed_in, weights):
        rows_buf, rowsT_buf, hidden_buf, y_buf = bufs
        n_blocks = blocks_of(L)
        groups = [range(g, min(g + GROUP, n_blocks)) for g in range(0, n_blocks, GROUP)]
        ld_rows = [Loads(nc, f"ld_rows{L}{i}") for i in range(2)]
        st_y = [Loads(nc, f"st_y{L}{i}") for i in range(2)]
        rows_free, y_free = [(), ()], [(), ()]
        rowsT_free = [(), ()]
        hidden_slots = Slots([hidden_buf[:, n, :, :] for n in range(3)])
        rows_in, flipped = {}, {}
        sp.wait(scattered)
        pe.wait(routed_in, named)
        act.wait(weights, named)
        dve.wait(routed_in)

        def load_rows(g):
            sp.wait(*rows_free[g % 2])
            b0, m = groups[g][0], len(groups[g])
            rows_in[g] = ld_rows[g % 2].did(sync.dma_start(
                rows_buf[:, g % 2, 0:m, :], routed_x[L][b0 * P:(b0 + m) * P, :].rearrange("(k p) d -> p k d", p=P)))

        def flip_rows(g):
            m = len(groups[g])
            w = m * P
            s, bank, free = small.take()
            pe.wait(*free, rows_in[g])
            for k in range(m):
                last = tensor.transpose(bank[:, k * P:(k + 1) * P], rows_buf[:, g % 2, k, :], ident[:, :])
            last = pe.did(last)
            rows_free[g % 2] = (last,)
            dve.wait(last, *rowsT_free[g % 2])
            flipped[g] = dve.did(vector.tensor_copy(rowsT_buf[:, g % 2, 0:w], bank[:, 0:w]))
            small.release(s, flipped[g])

        up = {}

        w1_free, w1_ready = [(), ()], {}

        def fetch_w1(b):
            e_dve = nc.values_load(block_expert[L][0:1, b:b + 1], engines=[mybir.EngineType.DVE], min_val=0, max_val=E - 1)
            dve.wait(*w1_free[b % 2])
            w1_ready[b] = dve.did(vector.tensor_copy(
                w1_block[:, b % 2, :], w1_all[:, bass.ds(e_dve, 1), :].rearrange("p o f -> p (o f)")))

        def up_block(b):
            g = b // GROUP
            k = b - groups[g][0]
            e_pe = nc.values_load(block_expert[L][0:1, b:b + 1], engines=[mybir.EngineType.PE], min_val=0, max_val=E - 1)
            e_act = nc.values_load(block_expert[L][0:1, b:b + 1], engines=[mybir.EngineType.Activation], min_val=0, max_val=E - 1)
            i, pair, free = pairs.take()
            pe.wait(*free, flipped[g], w1_ready[b])
            for j in range(FJ):
                last = tensor.matmul(pair[:, j * P:(j + 1) * P],
                                     w1_block[:, b % 2, j * P:(j + 1) * P],
                                     rowsT_buf[:, g % 2, k * P:(k + 1) * P], start=True, stop=True)
            last = pe.did(last)
            w1_free[b % 2] = (last,)
            if k == len(groups[g]) - 1:
                rowsT_free[g % 2] = (last,)
            hi, hidden, h_free = hidden_slots.take()
            act.wait(last, *h_free)
            for j in range(FJ):
                last = act.did(scalar.activation(hidden[:, j, :], pair[:, j * P:(j + 1) * P], func,
                                                 bias=b1[:, bass.ds(e_act, 1), j:j + 1].rearrange("p o f -> p (o f)")))
            pairs.release(i, last)
            up[b] = (hi, hidden, last, e_pe)

        y_bank = {}

        def down_block(b):
            g = b // GROUP
            k = b - groups[g][0]
            hi, hidden, h_ready, e_pe = up.pop(b)
            if k == 0:
                y_bank[g] = accum.take()
                pe.wait(*y_bank[g][2])
            i, bank, _ = y_bank[g]
            pe.wait(h_ready)
            for j in range(FJ):
                last = tensor.matmul(bank[:, k * D:(k + 1) * D], hidden[:, j, :],
                                     w2_all[:, bass.ds(e_pe, 1), j, :].rearrange("p o d -> p (o d)"),
                                     start=(j == 0), stop=(j == FJ - 1))
            last = pe.did(last)
            hidden_slots.release(hi, last)
            if k == len(groups[g]) - 1:
                m = len(groups[g])
                dve.wait(last, *y_free[g % 2])
                last = dve.did(vector.tensor_copy(y_buf[:, g % 2, 0:m, :], bank[:, 0:m * D].rearrange("p (k d) -> p k d", d=D)))
                accum.release(i, last)
                sp.wait(last)
                t = st_y[g % 2].did(sync.dma_start(
                    routed_y[L][groups[g][0] * P:(groups[g][0] + m) * P, :].rearrange("(k p) d -> p k d", p=P),
                    y_buf[:, g % 2, 0:m, :]))
                y_free[g % 2] = (t,)

        load_rows(0)
        load_rows(1)
        flip_rows(0)
        fetch_w1(0)
        fetch_w1(1)
        up_block(0)
        for b in range(n_blocks):
            g = b // GROUP
            if b + 1 < n_blocks:
                if (b + 1) % GROUP == GROUP // 2 and g + 1 < len(groups):
                    flip_rows(g + 1)
                    if g + 2 < len(groups):
                        load_rows(g + 2)
                up_block(b + 1)
            if b + 2 < n_blocks:
                fetch_w1(b + 2)
            down_block(b)
        return last_tick(pe), [y_free[0][0], y_free[1][0]]

    def last_tick(lane):
        return (lane.sem, lane.count)

    def gather_rows(L, k, target, stored, after):
        ld_picked = Loads(nc, f"ld_picked{L}{k}")
        pool.wait(*stored, *after)
        for t in range(NT):
            last = ld_picked.did(gpsimd.indirect_dma_start(
                out=target[:, t, :], out_offset=None, in_=routed_y[L][:, :],
                in_offset=bass.IndirectOffsetOnAxis(ap=slots_u[k][:, t:t + 1], axis=0)))
        return last

    def second_biases(L, mixT_ready, weights):
        n = E + L
        for c in range(NC):
            i, bank, free = accum.take()
            pe.wait(*free, mixT_ready, weights)
            for k in range(4):
                t = 4 * c + k
                last = tensor.matmul(bank[:, k * D:(k + 1) * D], mixT[0:n, t * P:(t + 1) * P], b2[0:n, :],
                                     start=True, stop=True)
            last = pe.did(last)
            dve.wait(last)
            last = dve.did(vector.tensor_copy(ffn[:, 4 * c:4 * c + 4, :], bank.rearrange("p (k d) -> p k d", d=D)))
            accum.release(i, last)
        return last

    def shared_ffn(hT, xnT_ready, weights, w_ready, biases_done):
        hT_slots = Slots([hT[:, n, :, :] for n in range(2)])
        act.wait(weights)
        pe.wait(xnT_ready, w_ready)
        dve.wait(biases_done)
        up = {}

        def project_up(c):
            hi, h, h_free = hT_slots.take()
            for half in range(FJ // 2):
                i, pair, free = pairs.take()
                pe.wait(*free)
                for jj in range(2):
                    j = 2 * half + jj
                    last = tensor.matmul(pair[:, jj * BANK:(jj + 1) * BANK], shared_w1[:, j * P:(j + 1) * P],
                                         xnT[:, c * BANK:(c + 1) * BANK], start=True, stop=True)
                last = pe.did(last)
                act.wait(last, *h_free)
                for jj in range(2):
                    j = 2 * half + jj
                    last = act.did(scalar.activation(h[:, j, :], pair[:, jj * BANK:(jj + 1) * BANK], ACT.Silu,
                                                     bias=b1[:, E, j:j + 1]))
                pairs.release(i, last)
            up[c] = (hi, h, last)

        def project_down(c):
            hi, h, h_ready = up.pop(c)
            i, bank, free = accum.take()
            pe.wait(*free, h_ready)
            for k in range(4):
                for j in range(FJ):
                    last = tensor.matmul(bank[:, k * D:(k + 1) * D], h[:, j, k * P:(k + 1) * P], shared_w2[:, j, :],
                                         start=(j == 0), stop=(j == FJ - 1))
            last = pe.did(last)
            hT_slots.release(hi, last)
            dve.wait(last)
            part = slice(4 * c, 4 * c + 4)
            last = dve.did(vector.scalar_tensor_tensor(
                out=ffn[:, part, :], in0=bank.rearrange("p (k d) -> p k d", d=D), scalar=SHARED,
                in1=ffn[:, part, :], op0=ALU.mult, op1=ALU.add))
            accum.release(i, last)
            return last

        project_up(0)
        for c in range(NC):
            if c + 1 < NC:
                project_up(c + 1)
            last = project_down(c)
        return last

    def gate(attn_ready, ffn_ready, store):
        done = []
        act.wait(ffn_ready)
        silu = [act.did(scalar.activation(ffn[:, 4 * c:4 * c + 4, :], ffn[:, 4 * c:4 * c + 4, :], ACT.Silu))
                for c in range(NC)]
        dve.wait(attn_ready)
        for c in range(NC):
            part = slice(4 * c, 4 * c + 4)
            dve.wait(silu[c])
            last = dve.did(vector.tensor_tensor(ffn[:, part, :], ffn[:, part, :], attn[:, part, :], ALU.mult))
            dve.wait(last)
            last = dve.did(vector.tensor_tensor(x[:, part, :], x[:, part, :], ffn[:, part, :], ALU.add))
            done.append(last)
            if store:
                sp.wait(last)
                st_out.did(sync.dma_start(out.rearrange("b (t p) d -> p (b t) d", p=P)[:, part, :], x[:, part, :]))
        return done

    def project_features(w, bias, target, func, scale, xnT_ready, weights, free):
        pe.wait(xnT_ready, weights)
        act.wait(weights)
        act.wait(*free)
        done = []
        for c in range(NC):
            i, bank, bank_free = accum.take()
            pe.wait(*bank_free)
            last = pe.did(tensor.matmul(bank, wqkvo[:, w, :], xnT[:, c * BANK:(c + 1) * BANK], start=True, stop=True))
            act.wait(last)
            last = act.did(scalar.activation(target[:, c * BANK:(c + 1) * BANK], bank, func, bias=bias))
            accum.release(i, last)
            done.append(last)
        return done

    def value_products(xnT_ready, weights):
        pe.wait(xnT_ready, weights)
        for c in range(NC):
            i, bank, free = accum.take()
            pe.wait(*free)
            for k in range(4):
                t = 4 * c + k
                last = tensor.matmul(bank[:, k * D:(k + 1) * D], xnT[:, t * P:(t + 1) * P], wqkvo[:, 2, :],
                                     start=True, stop=True)
            yield c, i, bank.rearrange("p (k d) -> p k d", d=D), pe.did(last)

    def bias_of(i):
        return bvo[:, i, :].unsqueeze(1).to_broadcast([P, 4, D])

    scope0 = [nc.sbuf_tensor(*s) for s in (
        ("qT", [P, T], FP32), ("kT", [P, T], FP32), ("v", [P, NT, D], FP32),
        ("causal", [P, S + (TPB - 1) * P], FP32), ("yT", [P, 2, P], FP32),
        ("scores", [P, 2, S], FP32), ("probs", [P, 3, S], FP32), ("probsT", [P, 2, S], FP32),
        ("l0_cols", [P, 4, NT], FP32), ("rows0", [P, 2, GROUP, D], FP32), ("rowsT0", [P, 2, BANK], FP32),
        ("hidden0", [P, 3, FJ, P], FP32), ("y0", [P, 2, GROUP, D], FP32), ("picked0", [P, NT, D], FP32))]
    qT, kT, v, causal, yT, scores, probs, probsT, l0_cols, rows0, rowsT0, hidden0, y0, picked0 = [s.__enter__() for s in scope0]

    t = pool.did(gpsimd.memset(causal[:, :], 0.0))
    pool.wait(t)
    causal_done = pool.did(gpsimd.affine_select(
        out=causal[:, :], in_=causal[:, :], compare_op=ALU.is_ge, fill=-NEG, base=(TPB - 1) * P,
        pattern=[[-1, S + (TPB - 1) * P]], channel_multiplier=1))

    weights = load_layer_weights(0)
    zeroed = zero_routed(0)
    routed_in = load_routed(0, ())
    normed, xnT_chunks = layernorm(x_in, (), ())
    xnT_ready = xnT_chunks[-1]

    t = router_logits(0, xnT_chunks, weights)
    mix_ready = one_hot_of_max(logits, mix[:, :, 0:E], rcol, rt1, t)
    mixT_ready = transpose_mix(E, mix_ready, ())
    placed, named = dispatch(0, [mix[:, :, 0:E]], mix_ready)
    scattered = scatter_rows(0, placed, normed[-1], zeroed)

    q_done = project_features(0, bqk[:, 0:1], qT, ACT.Relu, 1.0, xnT_ready, weights, ())
    k_done = project_features(1, bqk[:, 1:2], kT, ACT.Relu, 1.0, xnT_ready, weights, ())
    dve.wait(weights)
    for c, i, bank, t in value_products(xnT_ready, weights):
        dve.wait(t)
        part = slice(4 * c, 4 * c + 4)
        t = dve.did(vector.tensor_tensor(v[:, part, :], bank, bias_of(0), ALU.add))
        accum.release(i, t)
        dve.wait(t)
        v_done = dve.did(vector.tensor_relu(v[:, part, :], v[:, part, :]))

    neg_max, row_sum, inv_sum = (l0_cols[:, n, :] for n in range(3))
    dve.wait(causal_done)
    pe.wait(v_done, q_done[-1], k_done[-1])
    scaled, exped, transposed, multiplied = {}, {}, {}, {}

    def l0_scores(t):
        b, i = divmod(t, TPB)
        s, pair, free = pairs.take()
        pe.wait(*free)
        for c in range(S // BANK):
            last = tensor.matmul(pair[:, c * BANK:(c + 1) * BANK], qT[:, t * P:(t + 1) * P],
                                 kT[:, b * S + c * BANK:b * S + (c + 1) * BANK], start=True, stop=True)
        last = pe.did(last)
        dve.wait(last, exped.get(t - 2))
        lo = (TPB - 1 - i) * P
        last = dve.did(vector.scalar_tensor_tensor(
            out=scores[:, t % 2, :], in0=pair, scalar=1.0 / float(np.sqrt(np.float32(D))), in1=causal[:, lo:lo + S],
            op0=ALU.mult, op1=ALU.add))
        pairs.release(s, last)
        dve.wait(last)
        scaled[t] = dve.did(vector.tensor_reduce(neg_max[:, t:t + 1], scores[:, t % 2, :], AX.X, ALU.max, negate=True))
        act.wait(scaled[t], transposed.get(t - 3))
        exped[t] = act.did(scalar.activation(probs[:, t % 3, :], scores[:, t % 2, :], ACT.Exp,
                                             bias=neg_max[:, t:t + 1], accum_out=row_sum[:, t:t + 1]))

    probs_copied, y_copied, y_read = {}, {}, {}

    def l0_transposes(t):
        s, pair, free = pairs.take()
        pe.wait(*free, exped[t])
        for j in range(TPB):
            last = tensor.transpose(pair[:, j * P:(j + 1) * P], probs[:, t % 3, j * P:(j + 1) * P], ident[:, :])
        transposed[t] = pe.did(last)
        act.wait(transposed[t], multiplied.get(t - 2))
        probs_copied[t] = act.did(scalar.activation(probsT[:, t % 2, :], pair, ACT.Copy))
        pairs.release(s, probs_copied[t])

    def l0_values(t):
        b, i = divmod(t, TPB)
        s, bank, free = small.take()
        pe.wait(*free, probs_copied[t])
        for j in range(TPB):
            last = tensor.matmul(bank[:, 0:P], v[:, b * TPB + j, :], probsT[:, t % 2, j * P:(j + 1) * P],
                                 start=(j == 0), stop=(j == TPB - 1))
        multiplied[t] = pe.did(last)
        act.wait(multiplied[t], y_read.get(t - 2))
        y_copied[t] = act.did(scalar.activation(yT[:, t % 2, :], bank[:, 0:P], ACT.Copy))
        small.release(s, y_copied[t])

    def l0_output(t):
        s, bank, free = small.take()
        pe.wait(*free, y_copied[t])
        last = y_read[t] = pe.did(tensor.matmul(bank[:, 0:D], yT[:, t % 2, :], wqkvo[:, 3, :], start=True, stop=True))
        dve.wait(exped[t])
        r = dve.did(vector.reciprocal(inv_sum[:, t:t + 1], row_sum[:, t:t + 1]))
        dve.wait(last, r)
        last = dve.did(vector.scalar_tensor_tensor(
            out=attn[:, t, :], in0=bank[:, 0:D], scalar=inv_sum[:, t:t + 1], in1=bvo[:, 1, :],
            op0=ALU.mult, op1=ALU.add))
        small.release(s, last)
        dve.wait(last)
        return dve.did(vector.tensor_relu(attn[:, t, :], attn[:, t, :]))

    def l0_attention(b, beside=None):
        tiles = range(b * TPB, (b + 1) * TPB)
        l0_scores(tiles[0])
        l0_scores(tiles[1])
        for t in tiles:
            l0_transposes(t)
            if t + 2 in tiles:
                l0_scores(t + 2)
            l0_values(t)
            if t > tiles[0]:
                done = l0_output(t - 1)
            for step in (beside or {}).get(t - tiles[0], ()):
                step()
        return l0_output(tiles[-1])

    l0_attention(0)
    ffn_multiplied, stored = routed_ffn(0, ACT.Relu, (rows0, rowsT0, hidden0, y0), named, scattered, routed_in, weights)
    biases_done = second_biases(0, mixT_ready, weights)
    picked_in = gather_rows(0, 0, picked0, stored, ())
    routed_in1 = load_routed(1, (ffn_multiplied,))
    attn_ready = l0_attention(1)
    dve.wait(picked_in)
    for c in range(NC):
        part = slice(4 * c, 4 * c + 4)
        dve.wait(biases_done)
        ffn_ready = dve.did(vector.tensor_tensor(ffn[:, part, :], ffn[:, part, :], picked0[:, part, :], ALU.add))
    x_done = gate(attn_ready, ffn_ready, False)
    for s in reversed(scope0):
        s.__exit__(None, None, None)

    weights = load_layer_weights(1, x_done[-1])
    zeroed = zero_routed(1)
    shared_in = ld_shared.did(sync.dma_start(shared_w1[:, :], a["L1_W1"][E]))
    shared_in = ld_shared.did(sync.dma_start(shared_w2[:, :, :], a["L1_W2"][E].rearrange("(j p) d -> p j d", p=P)))
    normed, xnT_chunks = layernorm(x_done, (), (x_done[-1],))
    xnT_ready = xnT_chunks[-1]

    last = router_logits(1, xnT_chunks, weights)
    dve.wait(last)
    last = dve.did(vector.tensor_reduce(rcol[:, :], logits[:, :, :], AX.X, ALU.max))
    dve.wait(last)
    last = dve.did(vector.tensor_tensor(logits[:, :, :], logits[:, :, :], over_experts(rcol), ALU.subtract))
    act.wait(last)
    last = act.did(scalar.activation(logits[:, :, :], logits[:, :, :], ACT.Exp))
    dve.wait(last)
    last = dve.did(vector.tensor_reduce(rcol[:, :], logits[:, :, :], AX.X, ALU.add))
    dve.wait(last)
    last = dve.did(vector.reciprocal(rcol[:, :], rcol[:, :]))
    dve.wait(last)
    last = dve.did(vector.tensor_tensor(logits[:, :, :], logits[:, :, :], over_experts(rcol), ALU.mult))
    last = one_hot_of_max(logits, rt2[:, :, :], rcol, rt1, last)
    dve.wait(last)
    last = dve.did(vector.scalar_tensor_tensor(out=rt3[:, :, :], in0=rt2[:, :, :], scalar=-2.0, in1=logits[:, :, :],
                                               op0=ALU.mult, op1=ALU.add))
    last = one_hot_of_max(rt3, rt1[:, :, :], rcol2, rt1, last)
    placed, named = dispatch(1, [rt2[:, :, :], rt1[:, :, :]], last)
    dve.wait(placed)
    dve.wait(last)
    last = dve.did(vector.tensor_tensor(rt1[:, :, :], rt1[:, :, :], rt2[:, :, :], ALU.add))
    last2 = dve.did(vector.tensor_tensor(rcol3[:, :], rcol[:, :], rcol2[:, :], ALU.add))
    dve.wait(last, last2)
    last = dve.did(vector.tensor_tensor(rt1[:, :, :], rt1[:, :, :], logits[:, :, :], ALU.mult))
    last2 = dve.did(vector.tensor_scalar(rcol3[:, :], rcol3[:, :], TOPK_EPS, None, ALU.add))
    dve.wait(last2)
    last2 = dve.did(vector.reciprocal(rcol3[:, :], rcol3[:, :]))
    dve.wait(last, last2)
    dve.did(vector.tensor_tensor(weight1[:, :], rcol[:, :], rcol3[:, :], ALU.mult))
    dve.did(vector.tensor_tensor(weight2[:, :], rcol2[:, :], rcol3[:, :], ALU.mult))
    dve.did(vector.memset(mix[:, :, E:E + 1], SHARED))
    mix_ready = dve.did(vector.tensor_tensor(mix[:, :, 0:E], rt1[:, :, :], over_experts(rcol3), ALU.mult))
    mixT_ready = transpose_mix(E + 1, mix_ready, (x_done[-1],))

    scope1 = []

    def scoped(name, shape, dt=FP32):
        scope1.append(nc.sbuf_tensor(name, shape, dt))
        return scope1[-1].__enter__()

    v_aug = scoped("v_aug", [P, NT, H, V_COLS])
    bq_scaled = scoped("bq_scaled", [P, 1])
    head_sum = scoped("head_sum", [P, H])
    norm_max = scoped("norm_max", [H, 2, NC])
    batch_max = scoped("batch_max", [H, 2, B])
    span = scoped("span", [H, B])
    worst = scoped("worst", [H, 1])
    worst_row = scoped("worst_row", [1, 2])
    flag = scoped("flag", [1, 1], mybir.dt.int32)
    last_key = scoped("last_key", [P, B])
    far_limit = scoped("far_limit", [H, 1])
    RING = 4
    stacks = [[scoped(f"{w}_stack{n}", [P, S], BF16) for w in "qk"] for n in range(RING)]
    merged = scoped("merged", [P, 2, 4, D])
    mergedT = scoped("mergedT", [P, 2, BANK])
    row_max = scoped("row_max", [P, 2, TPB])
    neg_row_max = scoped("neg_row_max", [P, 2, TPB], BF16)
    neg_row_maxT = scoped("neg_row_maxT", [TPB, 2, P], BF16)
    recips = scoped("recips", [P, 2, 4, 4])
    arena = scoped("arena", [P, ARENA])
    arena_used = {}

    def carve(stage, shape, dt=FP32):
        n = int(np.prod(shape)) * (2 if dt == BF16 else 4) // 4
        at = arena_used.get(stage, 0)
        arena_used[stage] = at + n
        assert at + n <= ARENA
        view = arena[:, at:at + n]
        if dt == BF16:
            view = view.bitcast(BF16)
        names = "abc"[:len(shape)]
        return view.rearrange(f"p ({' '.join(names)}) -> p {' '.join(names)}", **dict(zip(names, shape)))

    proj, rest = (carve(0, [T]) for _ in range(2))
    parts = [carve(0, [T], BF16) for _ in range(PARTS)]
    squares = carve(0, [2, BANK])
    exps = carve(1, [4, 2 * BANK])
    heads_all = carve(1, [2 * (H // 4), BANK]).rearrange("p (q g) n -> p q g n", q=2)
    v_flat = v_aug[:, :, :, :].rearrange("p t h c -> p (t h c)")
    hT = v_flat[:, 0:2 * FJ * BANK].rearrange("p (n j c) -> p n j c", n=2, j=FJ)
    picked1 = v_flat[:, 2 * FJ * BANK:2 * FJ * BANK + T].rearrange("p (t d) -> p t d", d=D)
    rows1 = carve(2, [2, GROUP, D])
    rowsT1 = carve(2, [2, BANK])
    hidden1 = carve(2, [3, FJ, P])
    y1 = carve(2, [2, GROUP, D])
    split_dram = [nc.dram_tensor(f"split_{w}", [PARTS, P, T], BF16).ap() for w in "qk"]

    pool.wait(x_done[-1])
    for q_stack, k_stack in stacks:
        for buf in (q_stack, k_stack):
            pool.did(gpsimd.memset(buf[:, :], 0.0))
    stack_const = (pool.sem, pool.count)
    const_sem = Loads(nc, "ld_const")
    sp.wait(stack_const)
    for q_stack, k_stack in stacks:
        const_sem.did(sync.dma_start(q_stack[PROD_ROWS:PROD_ROWS + ALIBI_ROWS, :], a["ones_rows"].bitcast(BF16)))
        consts_in = const_sem.did(sync.dma_start(k_stack[MAX_ROW:MAX_ROW + 1, :], a["ones_rows"][0:1, :].bitcast(BF16)))

    split_sem = [Loads(nc, f"st_split_{w}") for w in "qk"]
    guard_sem = Loads(nc, "ld_guard")
    guard_in = guard_sem.did(sync.dma_start(head_sum[:, :], a["head_of"]))
    guard_in = guard_sem.did(sync.dma_start(far_limit[:, :], a["limits"]))
    dve.wait(weights)
    t = dve.did(vector.tensor_scalar(bq_scaled[:, :], bqk[:, 0:1], HD ** -0.5, None, ALU.mult))
    act.wait(t)
    split_done = []
    stored = ()
    squares_read = [None, None]
    for w, bias, scale, order in ((1, bqk[:, 1:2], 1.0, (1, 0, 3, 2)), (0, bq_scaled[:, 0:1], HD ** -0.5, (0, 1, 2, 3))):
        act.wait(*stored)
        pe.wait(xnT_ready, weights, guard_in)
        for c in order:
            cols = slice(c * BANK, (c + 1) * BANK)
            b = c // (NC // B)
            i, bank, bank_free = accum.take()
            pe.wait(*bank_free)
            last = pe.did(tensor.matmul(bank, wqkvo[:, w, :], xnT[:, cols], start=True, stop=True))
            act.wait(last)
            projected = act.did(scalar.activation(proj[:, cols], bank, ACT.Identity, bias=bias, scale=scale))
            accum.release(i, projected)
            dve.wait(projected, *stored)
            last = dve.did(vector.tensor_copy(parts[0][:, cols], proj[:, cols]))
            if w == 1 and order.index(c) % 2 == 0:
                act.wait(projected)
                act.wait(act.did(scalar.mul(last_key[:, b:b + 1], proj[:, (b + 1) * S - 1:(b + 1) * S], -1.0)))
            act.wait(projected, squares_read[c % 2])
            t = act.did(scalar.activation(squares[:, c % 2, :], proj[:, cols], ACT.Square,
                                          bias=last_key[:, b:b + 1] if w == 1 else 0.0))
            i, bank, bank_free = accum.take()
            pe.wait(*bank_free, t)
            t = squares_read[c % 2] = pe.did(tensor.matmul(bank[0:H, :], head_sum[:, :], squares[:, c % 2, :],
                                                           start=True, stop=True))
            for n in (1, 2):
                src = proj if n == 1 else rest
                dve.wait(last)
                last = dve.did(vector.tensor_tensor(rest[:, cols], src[:, cols], parts[n - 1][:, cols], ALU.subtract))
                dve.wait(last)
                last = dve.did(vector.tensor_copy(parts[n][:, cols], rest[:, cols]))
            dve.wait(t)
            widest = dve.did(vector.tensor_reduce(norm_max[:, w, c:c + 1], bank[0:H, :], AX.X, ALU.max))
            accum.release(i, widest)
        sp.wait(last)
        for n in range(PARTS):
            t = split_sem[w].did(sync.dma_start(split_dram[w][n], parts[n][:, :]))
        split_done.append(t)
        stored = (t,)

    dve.wait(widest, guard_in)
    last = dve.did(vector.tensor_reduce(
        batch_max[:, :, :], norm_max[:, :, :].rearrange("h w (b c) -> h w b c", b=B), AX.X, ALU.max))
    dve.wait(last)
    last = dve.did(vector.tensor_tensor(span[:, :], batch_max[:, 0, :], batch_max[:, 1, :], ALU.mult))
    dve.wait(last)
    last = dve.did(vector.tensor_reduce(worst[:, :], span[:, :], AX.X, ALU.max))
    dve.wait(last)
    last = dve.did(vector.tensor_tensor(worst[:, :], worst[:, :], far_limit[:, :], ALU.subtract))
    i, bank, bank_free = small.take()
    pe.wait(*bank_free, last)
    last = pe.did(tensor.transpose(bank[0:1, 0:H], worst[:, :], ident[0:H, 0:H]))
    dve.wait(last)
    last = dve.did(vector.tensor_reduce(worst_row[:, 0:1], bank[0:1, 0:H], AX.X, ALU.max))
    small.release(i, last)
    dve.wait(last)
    flagged = dve.did(vector.tensor_scalar(flag[:, :], worst_row[:, 0:1], 0.0, None, ALU.is_lt))

    t = pool.did(gpsimd.memset(v_aug[:, :, :, HD:V_COLS], 0.0))
    pool.wait(t)
    v_ones = pool.did(gpsimd.memset(v_aug[:, :, :, HD:HD + 1], 1.0))
    scattered = scatter_rows(1, placed, normed[-1], zeroed)
    dve.wait(weights)
    for c, i, bank, t in value_products(xnT_ready, weights):
        dve.wait(t)
        for k in range(4):
            v_done = dve.did(vector.tensor_tensor(
                v_aug[:, 4 * c + k, :, 0:HD], bank[:, k, :].rearrange("p (h d) -> p h d", d=HD),
                bvo[:, 0, :].rearrange("p (h d) -> p h d", d=HD), ALU.add))
        accum.release(i, v_done)

    def attention(arm, tiles):
        units = [(b, h) for b in range(B) for h in range(H)]
        stack_sem = [Loads(nc, f"ld_stack{n}{arm}") for n in range(RING)]
        max_sem = [Loads(nc, f"ld_max{n}{arm}") for n in range(RING)]
        stack_free = [() for _ in range(RING)]
        stack_in, max_in, maxed, max_flipped = {}, {}, {}, {}
        exp_slots = Slots([exps[:, n, :] for n in range(4)])
        out_bank = {}
        heads_read, heads_in = [None] * 2, [None] * 2
        merged_read, mergedT_read = [None] * 2, [None] * 2

        def load_stack(u):
            b, h = units[u]
            n = u % RING
            q_stack, k_stack = stacks[n]
            sp.wait(*stack_free[n])
            rows = PARTS * HD
            k0 = S - tiles[h] * P
            for i in range(PARTS):
                q_src = split_dram[0][i, h * HD:(h + 1) * HD, b * S:(b + 1) * S]
                k_src = split_dram[1][:, h * HD:(h + 1) * HD, b * S + k0:(b + 1) * S]
                stack_sem[n].did(sync.dma_start(
                    q_stack[i * rows:(i + 1) * rows, :], q_src.unsqueeze(0).to_broadcast([PARTS, HD, S])))
                stack_sem[n].did(sync.dma_start(k_stack[i * rows:(i + 1) * rows, k0:S], k_src))
            stack_in[u] = stack_sem[n].did(sync.dma_start(
                k_stack[PROD_ROWS:PROD_ROWS + ALIBI_ROWS, k0:S], a["alibi"][h, :, k0:S].bitcast(BF16)))

        def find_max(u):
            b, h = units[u]
            n, r = u % RING, u % 2
            q_stack, k_stack = stacks[n]
            keys = tiles[h] * P
            k0 = S - keys
            per_bank = BANK // keys
            fit = max(1, 2 * per_bank)

            def step(first):
                pe.wait(stack_in[u])
                s, pair, free = pairs.take()
                pe.wait(*free)
                for m in range(fit):
                    i = first + m
                    at = (m // per_bank) * BANK + (m % per_bank) * keys if per_bank else 0
                    for c in range(0, keys, BANK):
                        w = min(BANK, keys - c)
                        last = tensor.matmul(pair[:, at + c:at + c + w], q_stack[0:MAX_ROW, i * P:(i + 1) * P],
                                             k_stack[0:MAX_ROW, k0 + c:k0 + c + w], start=True, stop=True)
                last = pe.did(last)
                view, maxima = pair[:, 0:keys], row_max[:, r, first:first + fit]
                if per_bank:
                    view = pair.rearrange("p (g n) -> p g n", g=2)[:, :, 0:per_bank * keys]
                    view = view.rearrange("p g (m k) -> p g m k", k=keys)
                    maxima = maxima.rearrange("p (g m) -> p g m", g=2)
                dve.wait(last, max_flipped.get(u - 2))
                last = dve.did(vector.tensor_reduce(maxima, view, AX.X, ALU.max))
                pairs.release(s, last)
                if first + fit >= TPB:
                    dve.wait(last)
                    maxed[u] = dve.did(vector.tensor_scalar(neg_row_max[:, r, :], row_max[:, r, :], -1.0, None, ALU.mult))

            return [lambda first=first: step(first) for first in range(0, TPB, fit)]

        def place_max(u):
            n, r = u % RING, u % 2
            s, bank, free = small.take()
            pe.wait(*free, maxed[u])
            flipped = bank.bitcast(BF16)[0:TPB, 0:P]
            last = max_flipped[u] = pe.did(tensor.transpose(flipped, neg_row_max[:, r, :], ident_b[:, :]))
            dve.wait(last, max_in.get(u - 2))
            last = dve.did(vector.tensor_copy(neg_row_maxT[:, r, :], flipped))
            small.release(s, last)
            sp.wait(last)
            max_in[u] = max_sem[n].did(sync.dma_start(stacks[n][0][MAX_ROW:MAX_ROW + 1, :], neg_row_maxT[:, r, :]))

        def attend(u):
            b, h = units[u]
            n = u % RING
            q_stack, k_stack = stacks[n]
            quarter = h % 4
            kept = range(TPB - tiles[h], TPB)
            blocks = [(qc, j) for qc in range(S // BANK) for j in kept]
            ready = []

            def score(two):
                s, pair, free = pairs.take()
                pe.wait(*free, max_in[u])
                for m, (qc, j) in enumerate(two):
                    last = tensor.matmul(pair[:, m * BANK:(m + 1) * BANK], k_stack[0:MAX_ROW + 1, j * P:(j + 1) * P],
                                         q_stack[0:MAX_ROW + 1, qc * BANK:(qc + 1) * BANK], start=True, stop=True)
                last = pe.did(last)
                es, p_buf, p_free = exp_slots.take()
                act.wait(last, *p_free)
                t = act.did(scalar.activation(p_buf, pair, ACT.Exp))
                pairs.release(s, t)
                ready.append((two, es, p_buf, t))

            def multiply():
                two, es, p_buf, t = ready.pop(0)
                pe.wait(t)
                for m, (qc, j) in enumerate(two):
                    if quarter == 0 and j == kept[0]:
                        out_bank[qc] = accum.take()
                        pe.wait(*out_bank[qc][2])
                    slot, bank, _ = out_bank[qc]
                    last = tensor.matmul(bank[quarter * V_COLS:(quarter + 1) * V_COLS, :],
                                         v_aug[:, b * TPB + j, h, :], p_buf[:, m * BANK:(m + 1) * BANK],
                                         start=(j == kept[0]), stop=(j == kept[-1]),
                                         tile_position=(0, quarter * V_COLS))
                    if quarter == 3 and j == kept[-1]:
                        last = pe.did(last)
                        dve.wait(last, heads_read[qc])
                        t = dve.did(vector.tensor_copy(heads_all[:, qc, h // 4, :], bank))
                        accum.release(slot, t)
                        heads_in[qc] = t
                        last_tick = last
                        last = None
                last_tick = last_tick if last is None else pe.did(last)
                exp_slots.release(es, last_tick)
                stack_free[n] = (last_tick,)

            twos = [blocks[i:i + 2] for i in range(0, len(blocks), 2)]
            return [lambda two=two: score(two) for two in twos], multiply

        def merge(b, qc):
            for g in range(H // 4):
                s, bank, free = small.take()
                pe.wait(*free, heads_in[qc])
                for k in range(4):
                    last = tensor.transpose(bank[:, k * P:(k + 1) * P], heads_all[:, qc, g, k * P:(k + 1) * P], ident[:, :])
                last = heads_read[qc] = pe.did(last)
                by_head = bank.rearrange("p (k h c) -> p k h c", k=4, c=V_COLS)
                dve.wait(last)
                last = dve.did(vector.reciprocal(recips[:, g % 2, :, :], by_head[:, :, :, HD]))
                dve.wait(last, merged_read[qc])
                last = dve.did(vector.tensor_tensor(
                    merged[:, qc, :, g * 4 * HD:(g + 1) * 4 * HD].rearrange("p k (h d) -> p k h d", d=HD),
                    by_head[:, :, :, 0:HD], recips[:, g % 2, :, :].unsqueeze(3).to_broadcast([P, 4, 4, HD]), ALU.mult))
                small.release(s, last)
            s, bank, free = small.take()
            pe.wait(*free, last)
            for k in range(4):
                last = tensor.transpose(bank[:, k * P:(k + 1) * P], merged[:, qc, k, :], ident[:, :])
            last = merged_read[qc] = pe.did(last)
            act.wait(last, mergedT_read[qc])
            last = act.did(scalar.activation(mergedT[:, qc, :], bank, ACT.Copy))
            small.release(s, last)
            s, bank, free = small.take()
            pe.wait(*free, last)
            for k in range(4):
                last = tensor.matmul(bank[:, k * D:(k + 1) * D], mergedT[:, qc, k * P:(k + 1) * P], wqkvo[:, 3, :],
                                     start=True, stop=True)
            last = mergedT_read[qc] = pe.did(last)
            dve.wait(last)
            t0 = b * TPB + 4 * qc
            last = dve.did(vector.tensor_tensor(attn[:, t0:t0 + 4, :], bank.rearrange("p (k d) -> p k d", d=D), bias_of(1), ALU.add))
            small.release(s, last)

        load_stack(0)
        load_stack(1)
        load_stack(2)
        for step in find_max(0) + find_max(1):
            step()
        place_max(0)
        pending = []
        for u in range(len(units)):
            if u + 3 < len(units):
                load_stack(u + 3)
            if u + 1 < len(units):
                place_max(u + 1)
            searches = find_max(u + 2) if u + 2 < len(units) else []
            scores_, multiply = attend(u)
            share = -(-len(searches) // len(scores_)) if searches else 0
            for score in scores_:
                score()
                pending.append(multiply)
                for _ in range(share):
                    if searches:
                        searches.pop(0)()
                if len(pending) > 1:
                    pending.pop(0)()
            if units[u][1] == H - 1:
                while pending:
                    pending.pop(0)()
                for qc in range(S // BANK):
                    merge(units[u][0], qc)

    sp.wait(*split_done)
    sp.wait(scattered)
    pe.wait(consts_in, v_ones, v_done)
    rejoin("_l1")
    near = nc.values_load(flag[0:1, 0:1], min_val=0, max_val=1)
    with nc.If(near > 0):
        rejoin("_near", barrier=False)
        attention("_near", [near_tiles(h) for h in range(H)])
    with nc.Else():
        rejoin("_far", barrier=False)
        attention("_far", [TPB] * H)
    rejoin("_end")
    attn_ready = None
    _, stored = routed_ffn(1, ACT.Silu, (rows1, rowsT1, hidden1, y1), named, scattered, routed_in1, weights)
    picked_in = gather_rows(1, 0, picked1, stored, ())
    picked2_in = gather_rows(1, 1, xn, stored, ())
    biases_done = second_biases(1, mixT_ready, weights)
    ffn_ready = shared_ffn(hT, None, weights, shared_in, biases_done)
    for rows, column, t in ((picked1, weight1, picked_in), (xn, weight2, picked2_in)):
        dve.wait(t, ffn_ready)
        for t in range(NT):
            last = dve.did(vector.scalar_tensor_tensor(
                out=ffn[:, t, :], in0=rows[:, t, :], scalar=column[:, t:t + 1], in1=ffn[:, t, :],
                op0=ALU.mult, op1=ALU.add))
        ffn_ready = last
    gate(attn_ready, ffn_ready, True)
    sync.wait_ge(st_out.sem, st_out.count)
    for s in reversed(scope1):
        s.__exit__(None, None, None)


def split_constant(values):
    parts, rest = [], values.astype(np.float32)
    for _ in range(PARTS):
        part = (rest.view(np.uint32) & np.uint32(0xFFFF0000)).view(np.float32)
        parts.append((part.view(np.uint32) >> 16).astype(np.uint16))
        rest = rest - part
    return np.stack(parts)


def kernel(**inputs):
    import concourse.bacc as bacc
    from concourse.bass_utils import run_bass_kernel_spmd

    g = {k: np.asarray(v) for k, v in inputs.items()}
    arrays = {k: g[k] for k in g if "_attn_" in k}
    arrays["L0_ffn_br"] = g["L0_ffn_br"]
    arrays["L0_router"] = g["L0_ffn_Wr"].T
    arrays["L0_W1"] = g["L0_ffn_W1"].transpose(0, 2, 1)
    arrays["L0_W2"] = g["L0_ffn_W2"].transpose(0, 2, 1)
    arrays["L0_b1"], arrays["L0_b2"] = g["L0_ffn_b1"], g["L0_ffn_b2"]
    arrays["L1_router"] = g["L1_ffn_Wg"]
    for w in ("W1", "W2", "b1", "b2"):
        arrays[f"L1_{w}"] = np.concatenate([g[f"L1_ffn_{w}"], g[f"L1_ffn_{w[0]}s{w[1]}"][None]])
    for L in range(2):
        arrays[f"L{L}_b1"] = arrays[f"L{L}_b1"].reshape(E + L, FJ, P).transpose(2, 0, 1)
    slopes = 1.0 / 2.0 ** (np.arange(H, dtype=np.float32) / H)
    rel = slopes[:, None].astype(np.float32) * (np.arange(S, dtype=np.float32) - (S - 1))[None, :]
    arrays["alibi"] = np.ascontiguousarray(split_constant(rel).transpose(1, 0, 2))
    arrays["ones_rows"] = split_constant(np.ones((ALIBI_ROWS, S)))[0]
    arrays["head_of"] = np.kron(np.eye(H, dtype=np.float32), np.ones((HD, 1), np.float32))
    ids = np.arange(MAX_BLOCKS, dtype=np.float32)
    arrays["ids"] = np.broadcast_to(np.stack([ids, P * ids]), (P, 2, MAX_BLOCKS))
    arrays["limits"] = np.array([[(slope(h) * near_tiles(h) * P - UNDERFLOW) ** 2] for h in range(H)], np.float32)
    arrays = {k: np.ascontiguousarray(v) for k, v in arrays.items()}

    nc = bacc.Bacc("TRN2", target_bir_lowering=False, num_devices=1)
    aps = {k: nc.dram_tensor(k, v.shape, mybir.dt.from_np(v.dtype), kind="ExternalInput").ap() for k, v in arrays.items()}
    out = nc.dram_tensor("y", (B, S, D), FP32, kind="ExternalOutput").ap()
    build(nc, aps, out)
    r = run_bass_kernel_spmd(nc, [arrays], core_ids=[0])
    return r.results[0]["y"]
```

```python
import numpy as np

import concourse.bass as bass
from concourse import mybir

FP32 = mybir.dt.float32
BF16 = mybir.dt.bfloat16
ALU = mybir.AluOpType
ACT = mybir.ActivationFunctionType
AX = mybir.AxisListType

P = 128
B, S, D = 2, 1024, 128
T = B * S
NT = T // P
TPB = S // P
BANK = 512
NC = T // BANK
F, E = 512, 8
FJ = F // P
H, HD = 16, 8
NEG = 10000.0
EPS = 1e-5
TOPK_EPS = 1e-9
SHARED = 0.1

PARTS = 3
PROD_ROWS = PARTS * PARTS * HD
ALIBI_ROWS = PARTS
MAX_ROW = 96
V_COLS = 32


class Lane:

    def __init__(self, nc, engine, name):
        self.nc, self.e, self.name = nc, engine, name
        self.restart("")

    def restart(self, where):
        self.sem = self.nc.alloc_semaphore(self.name + where)
        self.count = 0
        self.seen = {}

    def did(self, instruction):
        self.count += 1
        instruction.then_inc(self.sem, 1)
        return (self.sem, self.count)

    def wait(self, *ticks):
        for tick in ticks:
            if tick is None:
                continue
            sem, value = tick
            if self.seen.get(sem.name, 0) < value:
                self.e.wait_ge(sem, value)
                self.seen[sem.name] = value


class Loads:

    def __init__(self, nc, name):
        self.sem = nc.alloc_semaphore(name)
        self.count = 0

    def did(self, instruction):
        self.count += 16
        instruction.then_inc(self.sem, 16)
        return (self.sem, self.count)


class Slots:

    def __init__(self, buffers):
        self.buffers = buffers
        self.free = [()] * len(buffers)
        self.n = 0

    def take(self):
        i = self.n % len(self.buffers)
        self.n += 1
        return i, self.buffers[i], self.free[i]

    def release(self, i, *ticks):
        self.free[i] = ticks

    def restart(self, buffers=None):
        self.buffers = buffers or self.buffers
        self.free = [()] * len(self.buffers)
        self.n = 0


UNDERFLOW = 105.0


def slope(h):
    return 1.0 / 2.0 ** (h / H)


def near_tiles(h):
    return 2 if slope(h) * 2 * P - UNDERFLOW > 68 else 3


def blocks_of(L):
    return (L + 1) * NT + E - 1


MAX_BLOCKS = 48
GROUP = BANK // P
ARENA = 8192


def build(nc, a, out):
    pe = Lane(nc, nc.tensor, "pe_done")
    act = Lane(nc, nc.scalar, "act_done")
    dve = Lane(nc, nc.vector, "dve_done")
    pool = Lane(nc, nc.gpsimd, "pool_done")
    sp = Lane(nc, nc.sync, "sp_done")
    tensor, scalar, vector, gpsimd, sync = nc.tensor, nc.scalar, nc.vector, nc.gpsimd, nc.sync

    def sb(name, shape, dt=FP32):
        return nc.alloc_sbuf_tensor(name, shape, dt)

    x = sb("x", [P, NT, D])
    xn = sb("xn", [P, NT, D])
    xnT = sb("xnT", [P, T])
    attn = sb("attn", [P, NT, D])
    ffn = sb("ffn", [P, NT, D])
    ident = sb("ident", [P, P])
    ident_b = sb("ident_b", [P, P], BF16)
    stats = sb("stats", [P, NT, 6])
    mv = sb("mv", [P, NT, 2])
    std = sb("std", [P, NT])
    rstd = sb("rstd", [P, NT])
    eps = sb("eps", [P, 1])
    wqkvo = sb("wqkvo", [P, 2, 4, D])
    bqk = sb("bqk", [P, 2, 2])
    bvo = sb("bvo", [P, 2, 2, D])
    router_w = sb("router_w", [P, 2, E])
    router_b = sb("router_b", [P, E])
    logits = sb("logits", [P, NT, E])
    mix = sb("mix", [P, NT, E + 1])
    mixT = sb("mixT", [E + 1, T])
    rt1 = sb("rt1", [P, NT, E])
    rt2 = sb("rt2", [P, NT, E])
    rt3 = sb("rt3", [P, NT, E])
    rcol = sb("rcol", [P, NT])
    rcol2 = sb("rcol2", [P, NT])
    rcol3 = sb("rcol3", [P, NT])
    weight1 = sb("weight1", [P, NT])
    weight2 = sb("weight2", [P, NT])
    first_rank = sb("first_rank", [P, E])
    b1 = sb("b1", [P, 2, E + 1, FJ])
    b2 = sb("b2", [E + 1, 2, D])
    w1_all = sb("w1_all", [P, E, F])
    w1_block = sb("w1_block", [P, 2, F])
    w2_all = sb("w2_all", [P, E, FJ, D])
    shared_w1 = sb("shared_w1", [P, F])
    shared_w2 = sb("shared_w2", [P, FJ, D])
    ones_f = sb("ones_f", [P, NT * E])
    ones_b = sb("ones_b", [P, P], BF16)
    before = sb("before", [P, P], BF16)
    ids = sb("numbers", [P, 2, MAX_BLOCKS])
    chosen = sb("chosen", [P, E, NT], BF16)
    in_tile = sb("in_tile", [P, E, NT])
    upto = sb("upto", [P, E, NT])
    place = sb("place", [P, E, NT])
    by_expert = sb("by_expert", [P, 6, E + 1])
    over = sb("over", [P, E, NT])
    product = sb("product", [P, E, NT])
    slot_f = sb("slot_f", [P, NT])
    slots_u = [sb(f"slots{i}", [P, NT], mybir.dt.uint32) for i in range(2)]
    past = sb("past", [1, MAX_BLOCKS, E])
    block_f = sb("block_f", [1, MAX_BLOCKS])
    block_expert = [sb(f"block_expert{L}", [1, MAX_BLOCKS], mybir.dt.int32) for L in range(2)]
    zeros = sb("zeros", [P, 4 * D])
    routed_x = [nc.dram_tensor(f"routed_x{L}", [blocks_of(L) * P, D], FP32).ap() for L in range(2)]
    routed_y = [nc.dram_tensor(f"routed_y{L}", [blocks_of(L) * P, D], FP32).ap() for L in range(2)]

    bq_scaled = sb("bq_scaled", [P, 1])
    head_sum = sb("head_sum", [P, H])
    norm_max = sb("norm_max", [H, 2, NC])
    batch_max = sb("batch_max", [H, 2, B])
    span = sb("span", [H, B])
    worst = sb("worst", [H, 1])
    worst_row = sb("worst_row", [1, 2])
    flag = sb("flag", [1, 1], mybir.dt.int32)
    last_key = sb("last_key", [P, B])
    far_limit = sb("far_limit", [H, 1])
    q_split = nc.dram_tensor("q_split", [H, PARTS * HD, T], BF16).ap()
    k_split = nc.dram_tensor("k_split", [H, PROD_ROWS + ALIBI_ROWS, T], BF16).ap()
    arena = sb("arena", [P, ARENA])
    arena_used = {}

    def carve(stage, shape, dt=FP32):
        n = int(np.prod(shape)) * (2 if dt == BF16 else 4) // 4
        at = arena_used.get(stage, 0)
        arena_used[stage] = at + n
        assert at + n <= ARENA
        view = arena[:, at:at + n]
        if dt == BF16:
            view = view.bitcast(BF16)
        names = "abc"[:len(shape)]
        return view.rearrange(f"p ({' '.join(names)}) -> p {' '.join(names)}", **dict(zip(names, shape)))

    ffn_shapes = ([2, GROUP, D], [2, BANK], [3, FJ, P], [2, GROUP, D])

    psum = nc.alloc_psum_tensor("psum", [P, 8 * BANK], FP32)
    pairs = Slots([psum[:, 2 * BANK:4 * BANK], psum[:, 4 * BANK:6 * BANK]])
    banks = [psum[:, n * BANK:(n + 1) * BANK] for n in range(8)]
    small = Slots(banks[0:2])
    accum = Slots(banks[6:8])

    def rejoin(where, barrier=True):
        if barrier:
            nc.all_engine_barrier()
        for lane in (pe, act, dve, pool, sp):
            lane.restart(where)
        for slots in (pairs, small, accum):
            slots.restart()

    ld_x = [Loads(nc, f"ld_x{c}") for c in range(NC)]
    ld_routed = [Loads(nc, f"ld_routed{L}") for L in range(2)]
    ld_shared = Loads(nc, "ld_shared")
    st_zero = [Loads(nc, f"st_zero{L}") for L in range(2)]
    st_out = Loads(nc, "st_out")

    pool.did(gpsimd.memset(ident[:, :], 0.0))
    t = pool.did(gpsimd.memset(ident_b[:, :], 0.0))
    pool.wait(t)
    for m in (ident, ident_b):
        ident_done = pool.did(gpsimd.affine_select(
            out=m[:, :], in_=m[:, :], compare_op=ALU.not_equal, fill=1.0, base=0,
            pattern=[[-1, P]], channel_multiplier=1))
    for e in range(E):
        rank_done = pool.did(gpsimd.memset(first_rank[:, e:e + 1], float(E - e)))
    eps_done = pool.did(gpsimd.memset(eps[:, :], EPS))
    zeros_done = pool.did(gpsimd.memset(zeros[:, :], 0.0))
    pool.did(gpsimd.memset(ones_f[:, :], 1.0))
    pool.did(gpsimd.memset(ones_b[:, :], 1.0))
    t = pool.did(gpsimd.memset(before[:, :], 1.0))
    pool.wait(t)
    counting_done = pool.did(gpsimd.affine_select(
        out=before[:, :], in_=before[:, :], compare_op=ALU.is_gt, fill=0.0, base=0,
        pattern=[[1, P]], channel_multiplier=-1))

    ids_in = Loads(nc, "ld_ids").did(sync.dma_start(ids[:, :, :], a["ids"]))
    x_dram = a["L0_attn_x"].rearrange("b (t p) d -> p (b t) d", p=P)
    x_in = []
    for c in range(NC):
        x_in.append(ld_x[c].did(sync.dma_start(x[:, 4 * c:4 * c + 4, :], x_dram[:, 4 * c:4 * c + 4, :])))

    def load_layer_weights(L):
        ld = Loads(nc, f"ld_w{L}")
        for i, w in enumerate(("Wq", "Wk", "Wv", "Wo")):
            ld.did(sync.dma_start(wqkvo[:, L, i, :], a[f"L{L}_attn_{w}"]))
        for i, w in enumerate(("bq", "bk")):
            ld.did(sync.dma_start(bqk[:, L, i:i + 1], a[f"L{L}_attn_{w}"].rearrange("(p o) -> p o", o=1)))
        for i, w in enumerate(("bv", "bo")):
            ld.did(sync.dma_start(bvo[:, L, i, :], a[f"L{L}_attn_{w}"].partition_broadcast(P)))
        ld.did(sync.dma_start(router_w[:, L, :], a[f"L{L}_router"]))
        if L == 0:
            ld.did(sync.dma_start(router_b[:, :], a["L0_ffn_br"].partition_broadcast(P)))
        n = E + L
        ld.did(sync.dma_start(b1[:, L, 0:n, :], a[f"L{L}_b1"]))
        return ld.did(sync.dma_start(b2[0:n, L, :], a[f"L{L}_b2"]))

    def zero_routed(L):
        sp.wait(zeros_done)
        n = blocks_of(L)
        for g in range(0, n, GROUP):
            m = min(GROUP, n - g)
            t = st_zero[L].did(sync.dma_start(
                routed_x[L][g * P:(g + m) * P, :].rearrange("(k p) d -> p k d", p=P),
                zeros[:, 0:m * D].rearrange("p (k d) -> p k d", d=D)))
        return t

    def load_routed(L, after):
        sp.wait(*after)
        ld_routed[L].did(sync.dma_start(w1_all[:, :, :], a[f"L{L}_W1"][0:E].rearrange("e d f -> d e f")))
        return ld_routed[L].did(sync.dma_start(w2_all[:, :, :, :].rearrange("p e j d -> p (e j) d"),
                                               a[f"L{L}_W2"][0:E].rearrange("e (j p) d -> p (e j) d", p=P)))

    def norm_stats(chunks, ready):
        tiles = range(4 * chunks[0], 4 * chunks[-1] + 4)
        for t in tiles:
            dve.wait(ready[t // 4])
            last = dve.did(vector.bn_stats(stats[:, t, :], x[:, t, :]))
        dve.wait(last)
        for t in tiles:
            last = dve.did(vector.bn_aggr(mv[:, t, :], stats[:, t, :]))
        return last

    def norm_root(chunks, counted):
        part = slice(4 * chunks[0], 4 * chunks[-1] + 4)
        act.wait(counted, eps_done)
        return act.did(scalar.activation(std[:, part], mv[:, part, 1], ACT.Sqrt, bias=eps[:, 0:1]))

    def norm_apply(chunks, std_done):
        part = slice(4 * chunks[0], 4 * chunks[-1] + 4)
        dve.wait(std_done)
        last = dve.did(vector.reciprocal(rstd[:, part], std[:, part]))
        dve.wait(last)
        normed = {}
        for c in chunks:
            for t in range(4 * c, 4 * c + 4):
                normed[c] = dve.did(vector.tensor_scalar(
                    xn[:, t, :], x[:, t, :], mv[:, t, 0:1], rstd[:, t:t + 1], ALU.subtract, ALU.mult))
        return normed

    def flip_xn(c, normed):
        i, bank, free = small.take()
        pe.wait(*free, normed, ident_done)
        for k in range(4):
            last = tensor.transpose(bank[:, k * P:(k + 1) * P], xn[:, 4 * c + k, :], ident[:, :])
        last = pe.did(last)
        act.wait(last)
        last = act.did(scalar.activation(xnT[:, c * BANK:(c + 1) * BANK], bank, ACT.Copy))
        small.release(i, last)
        return last

    def router_logits(L, xnT_ready, weights):
        i, bank, free = small.take()
        pe.wait(*free, weights, *xnT_ready)
        for t in range(NT):
            last = tensor.matmul(bank[:, t * E:(t + 1) * E], xnT[:, t * P:(t + 1) * P], router_w[:, L, :],
                                 start=True, stop=True)
        last = pe.did(last)
        dve.wait(last)
        flat = bank[:, 0:NT * E].rearrange("p (t e) -> p t e", e=E)
        if L == 0:
            dve.wait(weights)
            last = dve.did(vector.tensor_tensor(
                logits[:, :, :], flat, router_b[:, :].unsqueeze(1).to_broadcast([P, NT, E]), ALU.add))
        else:
            last = dve.did(vector.tensor_copy(logits[:, :, :], flat))
        small.release(i, last)
        return last

    def over_experts(col):
        return col[:, :].unsqueeze(2).to_broadcast([P, NT, E])

    def one_hot_of_max(values, onehot, top, work, ready):
        dve.wait(ready)
        last = dve.did(vector.tensor_reduce(top[:, :], values[:, :, :], AX.X, ALU.max))
        yield
        dve.wait(last)
        last = dve.did(vector.tensor_tensor(work[:, :, :], values[:, :, :], over_experts(top), ALU.is_equal))
        dve.wait(last, rank_done)
        last = dve.did(vector.tensor_tensor(
            work[:, :, :], work[:, :, :], first_rank[:, :].unsqueeze(1).to_broadcast([P, NT, E]), ALU.mult))
        dve.wait(last)
        yield
        last = dve.did(vector.tensor_reduce(rcol3[:, :], work[:, :, :], AX.X, ALU.max))
        dve.wait(last)
        return dve.did(vector.tensor_tensor(onehot, work[:, :, :], over_experts(rcol3), ALU.is_equal))

    def transpose_mix(n, ready, free_mixT):
        act.wait(*free_mixT)
        for c in range(NC):
            i, bank, free = small.take()
            pe.wait(*free, ready)
            for k in range(4):
                last = tensor.transpose(bank[0:n, k * P:(k + 1) * P], mix[:, 4 * c + k, 0:n], ident[:, :])
            last = pe.did(last)
            act.wait(last)
            last = act.did(scalar.activation(mixT[0:n, c * BANK:(c + 1) * BANK], bank[0:n, :], ACT.Copy))
            small.release(i, last)
            yield
        return last

    def dispatch(L, onehots, ready):
        n_blocks = blocks_of(L)
        by = "p e t -> p t e"
        as_et = [o.rearrange("p t e -> p e t") for o in onehots]
        dve.wait(ready, counting_done, ids_in)
        if L == 0:
            last = dve.did(vector.tensor_copy(chosen[:, :, :], as_et[0]))
        else:
            last = dve.did(vector.tensor_tensor(chosen[:, :, :], as_et[0], as_et[1], ALU.add))
        yield
        i, bank, free = small.take()
        pe.wait(*free, last)
        n = E * NT
        flat = chosen[:, :, :].rearrange("p e t -> p (e t)")
        tensor.matmul(bank[:, 0:n], before[:, :], flat, start=True, stop=True)
        last = pe.did(tensor.matmul(bank[:, n:2 * n], ones_b[:, :], flat, start=True, stop=True))
        rank = bank[:, 0:n].rearrange("p (e t) -> p e t", t=NT)
        dve.wait(last)
        last = dve.did(vector.tensor_copy(in_tile[:, :, :], bank[:, n:2 * n].rearrange("p (e t) -> p e t", t=NT)))
        ranked = dve.did(vector.tensor_copy(place[:, :, :], rank))
        small.release(i, ranked)
        yield
        dve.wait(last)
        last = dve.did(vector.tensor_tensor_scan(
            upto[:, :, :].rearrange("p e t -> p (e t)"), ones_f[:, :],
            in_tile[:, :, :].rearrange("p e t -> p (e t)"), 0.0, ALU.mult, ALU.add))
        cum, count, n_blk, end, base = (by_expert[:, m, :] for m in range(5))
        t = dve.did(vector.memset(by_expert[:, :, 0:1], 0.0))
        dve.wait(last, t)
        last = dve.did(vector.tensor_copy(cum[:, 1:E + 1], upto[:, :, NT - 1]))
        yield
        dve.wait(last)
        last = dve.did(vector.tensor_tensor(count[:, 1:E + 1], cum[:, 1:E + 1], cum[:, 0:E], ALU.subtract))
        dve.wait(last)
        last = dve.did(vector.tensor_tensor(
            over[:, :, :], count[:, 1:E + 1].unsqueeze(2).to_broadcast([P, E, NT]),
            ids[:, 1, 0:NT].unsqueeze(1).to_broadcast([P, E, NT]), ALU.is_gt))
        yield
        dve.wait(last)
        last = dve.did(vector.tensor_reduce(n_blk[:, 1:E + 1], over[:, :, :], AX.X, ALU.add))
        dve.wait(last)
        last = dve.did(vector.tensor_tensor_scan(end[:, 1:E + 1], ones_f[:, 0:E], n_blk[:, 1:E + 1], 0.0, ALU.mult, ALU.add))
        dve.wait(last)
        last = dve.did(vector.scalar_tensor_tensor(out=base[:, 0:E], in0=end[:, 0:E], scalar=float(P), in1=cum[:, 0:E],
                                                   op0=ALU.mult, op1=ALU.subtract))
        t = dve.did(vector.tensor_tensor(upto[:, :, :], upto[:, :, :], in_tile[:, :, :], ALU.subtract))
        yield
        dve.wait(t, ranked)
        t = dve.did(vector.tensor_tensor(place[:, :, :], place[:, :, :], upto[:, :, :], ALU.add))
        dve.wait(t, last)
        last = dve.did(vector.tensor_tensor(
            place[:, :, :], place[:, :, :], base[:, 0:E].unsqueeze(2).to_broadcast([P, E, NT]), ALU.add))
        for k, o in enumerate(as_et):
            yield
            dve.wait(last)
            last = dve.did(vector.tensor_tensor(product[:, :, :], place[:, :, :], o, ALU.mult))
            dve.wait(last)
            last = dve.did(vector.tensor_reduce(slot_f[:, :], product[:, :, :].rearrange(by), AX.X, ALU.add))
            dve.wait(last)
            placed = last = dve.did(vector.tensor_copy(slots_u[k][:, :], slot_f[:, :]))
        yield
        last = dve.did(vector.tensor_tensor(
            past[:, 0:n_blocks, :], end[0:1, 1:E + 1].unsqueeze(1).to_broadcast([1, n_blocks, E]),
            ids[0:1, 0, 0:n_blocks].unsqueeze(2).to_broadcast([1, n_blocks, E]), ALU.is_le))
        dve.wait(last)
        last = dve.did(vector.tensor_reduce(block_f[:, 0:n_blocks], past[:, 0:n_blocks, :], AX.X, ALU.add))
        dve.wait(last)
        named = dve.did(vector.tensor_scalar(block_expert[L][:, 0:n_blocks], block_f[:, 0:n_blocks], float(E - 1), None, ALU.min))
        return placed, named

    st_rows = [Loads(nc, f"st_rows{L}") for L in range(2)]

    def scatter_rows(L, placed, normed, zeroed):
        pool.wait(placed, zeroed, *normed)
        for k in range(L + 1):
            for t in range(NT):
                last = st_rows[L].did(gpsimd.indirect_dma_start(
                    out=routed_x[L][:, :], out_offset=bass.IndirectOffsetOnAxis(ap=slots_u[k][:, t:t + 1], axis=0),
                    in_=xn[:, t, :], in_offset=None))
        return last

    def routed_ffn(L, func, bufs, named, scattered, routed_in, weights):
        rows_buf, rowsT_buf, hidden_buf, y_buf = bufs
        n_blocks = blocks_of(L)
        groups = [range(g, min(g + GROUP, n_blocks)) for g in range(0, n_blocks, GROUP)]
        ld_rows = [Loads(nc, f"ld_rows{L}{i}") for i in range(2)]
        st_y = [Loads(nc, f"st_y{L}{i}") for i in range(2)]
        rows_free, y_free = [(), ()], [(), ()]
        rowsT_free = [(), ()]
        hidden_slots = Slots([hidden_buf[:, n, :, :] for n in range(3)])
        rows_in, flipped = {}, {}
        sp.wait(scattered)
        pe.wait(routed_in, named)
        act.wait(weights, named)
        dve.wait(routed_in)

        def load_rows(g):
            sp.wait(*rows_free[g % 2])
            b0, m = groups[g][0], len(groups[g])
            rows_in[g] = ld_rows[g % 2].did(sync.dma_start(
                rows_buf[:, g % 2, 0:m, :], routed_x[L][b0 * P:(b0 + m) * P, :].rearrange("(k p) d -> p k d", p=P)))

        def flip_rows(g):
            m = len(groups[g])
            w = m * P
            s, bank, free = small.take()
            pe.wait(*free, rows_in[g])
            for k in range(m):
                last = tensor.transpose(bank[:, k * P:(k + 1) * P], rows_buf[:, g % 2, k, :], ident[:, :])
            last = pe.did(last)
            rows_free[g % 2] = (last,)
            dve.wait(last, *rowsT_free[g % 2])
            flipped[g] = dve.did(vector.tensor_copy(rowsT_buf[:, g % 2, 0:w], bank[:, 0:w]))
            small.release(s, flipped[g])

        up = {}

        w1_free, w1_ready = [(), ()], {}

        def fetch_w1(b):
            e_dve = nc.values_load(block_expert[L][0:1, b:b + 1], engines=[mybir.EngineType.DVE], min_val=0, max_val=E - 1)
            dve.wait(*w1_free[b % 2])
            w1_ready[b] = dve.did(vector.tensor_copy(
                w1_block[:, b % 2, :], w1_all[:, bass.ds(e_dve, 1), :].rearrange("p o f -> p (o f)")))

        def up_block(b):
            g = b // GROUP
            k = b - groups[g][0]
            e_pe = nc.values_load(block_expert[L][0:1, b:b + 1], engines=[mybir.EngineType.PE], min_val=0, max_val=E - 1)
            e_act = nc.values_load(block_expert[L][0:1, b:b + 1], engines=[mybir.EngineType.Activation], min_val=0, max_val=E - 1)
            i, pair, free = pairs.take()
            pe.wait(*free, flipped[g], w1_ready[b])
            for j in range(FJ):
                last = tensor.matmul(pair[:, j * P:(j + 1) * P],
                                     w1_block[:, b % 2, j * P:(j + 1) * P],
                                     rowsT_buf[:, g % 2, k * P:(k + 1) * P], start=True, stop=True)
            last = pe.did(last)
            w1_free[b % 2] = (last,)
            if k == len(groups[g]) - 1:
                rowsT_free[g % 2] = (last,)
            hi, hidden, h_free = hidden_slots.take()
            act.wait(last, *h_free)
            for j in range(FJ):
                last = act.did(scalar.activation(hidden[:, j, :], pair[:, j * P:(j + 1) * P], func,
                                                 bias=b1[:, L, bass.ds(e_act, 1), j:j + 1].rearrange("p o f -> p (o f)")))
            pairs.release(i, last)
            up[b] = (hi, hidden, last, e_pe)

        y_bank = {}

        def down_block(b):
            g = b // GROUP
            k = b - groups[g][0]
            hi, hidden, h_ready, e_pe = up.pop(b)
            if k == 0:
                y_bank[g] = accum.take()
                pe.wait(*y_bank[g][2])
            i, bank, _ = y_bank[g]
            pe.wait(h_ready)
            for j in range(FJ):
                last = tensor.matmul(bank[:, k * D:(k + 1) * D], hidden[:, j, :],
                                     w2_all[:, bass.ds(e_pe, 1), j, :].rearrange("p o d -> p (o d)"),
                                     start=(j == 0), stop=(j == FJ - 1))
            last = pe.did(last)
            hidden_slots.release(hi, last)
            if k == len(groups[g]) - 1:
                m = len(groups[g])
                dve.wait(last, *y_free[g % 2])
                last = dve.did(vector.tensor_copy(y_buf[:, g % 2, 0:m, :], bank[:, 0:m * D].rearrange("p (k d) -> p k d", d=D)))
                accum.release(i, last)
                sp.wait(last)
                t = st_y[g % 2].did(sync.dma_start(
                    routed_y[L][groups[g][0] * P:(groups[g][0] + m) * P, :].rearrange("(k p) d -> p k d", p=P),
                    y_buf[:, g % 2, 0:m, :]))
                y_free[g % 2] = (t,)

        load_rows(0)
        load_rows(1)
        flip_rows(0)
        fetch_w1(0)
        fetch_w1(1)
        up_block(0)
        for b in range(n_blocks):
            g = b // GROUP
            if b + 1 < n_blocks:
                if (b + 1) % GROUP == GROUP // 2 and g + 1 < len(groups):
                    flip_rows(g + 1)
                    if g + 2 < len(groups):
                        load_rows(g + 2)
                up_block(b + 1)
            if b + 2 < n_blocks:
                fetch_w1(b + 2)
            down_block(b)
        return last_tick(pe), [y_free[0][0], y_free[1][0]]

    def run(steps):
        while True:
            try:
                next(steps)
            except StopIteration as end:
                return end.value

    def last_tick(lane):
        return (lane.sem, lane.count)

    def gather_rows(L, k, b, target, stored, after):
        pool.wait(*stored, *after)
        ld_picked = Loads(nc, f"ld_picked{L}{k}{b}")
        for t in range(b * TPB, (b + 1) * TPB):
            last = ld_picked.did(gpsimd.indirect_dma_start(
                out=target[:, t, :], out_offset=None, in_=routed_y[L][:, :],
                in_offset=bass.IndirectOffsetOnAxis(ap=slots_u[k][:, t:t + 1], axis=0)))
        return last

    def second_biases(L, mixT_ready, weights):
        n = E + L
        for c in range(NC):
            i, bank, free = accum.take()
            pe.wait(*free, mixT_ready, weights)
            for k in range(4):
                t = 4 * c + k
                last = tensor.matmul(bank[:, k * D:(k + 1) * D], mixT[0:n, t * P:(t + 1) * P], b2[0:n, L, :],
                                     start=True, stop=True)
            last = pe.did(last)
            dve.wait(last)
            last = dve.did(vector.tensor_copy(ffn[:, 4 * c:4 * c + 4, :], bank.rearrange("p (k d) -> p k d", d=D)))
            accum.release(i, last)
        return last

    def shared_ffn(hT, xnT_ready, weights, w_ready, biases_done, behind):
        hT_slots = Slots([hT[:, n, :, :] for n in range(2)])
        act.wait(weights)
        pe.wait(xnT_ready, w_ready)
        dve.wait(biases_done)
        up = {}

        def project_up(c):
            hi, h, h_free = hT_slots.take()
            for half in range(FJ // 2):
                i, pair, free = pairs.take()
                pe.wait(*free)
                for jj in range(2):
                    j = 2 * half + jj
                    last = tensor.matmul(pair[:, jj * BANK:(jj + 1) * BANK], shared_w1[:, j * P:(j + 1) * P],
                                         xnT[:, c * BANK:(c + 1) * BANK], start=True, stop=True)
                last = pe.did(last)
                act.wait(last, *h_free)
                for jj in range(2):
                    j = 2 * half + jj
                    last = act.did(scalar.activation(h[:, j, :], pair[:, jj * BANK:(jj + 1) * BANK], ACT.Silu,
                                                     bias=b1[:, 1, E, j:j + 1]))
                pairs.release(i, last)
            up[c] = (hi, h, last)

        def project_down(c):
            hi, h, h_ready = up.pop(c)
            i, bank, free = accum.take()
            pe.wait(*free, h_ready)
            for k in range(4):
                for j in range(FJ):
                    last = tensor.matmul(bank[:, k * D:(k + 1) * D], h[:, j, k * P:(k + 1) * P], shared_w2[:, j, :],
                                         start=(j == 0), stop=(j == FJ - 1))
            last = pe.did(last)
            hT_slots.release(hi, last)
            dve.wait(last)
            part = slice(4 * c, 4 * c + 4)
            last = dve.did(vector.scalar_tensor_tensor(
                out=ffn[:, part, :], in0=bank.rearrange("p (k d) -> p k d", d=D), scalar=SHARED,
                in1=ffn[:, part, :], op0=ALU.mult, op1=ALU.add))
            accum.release(i, last)
            return last

        project_up(0)
        for c in range(NC):
            if c + 1 < NC:
                project_up(c + 1)
            project_down(c)
            behind(c)

    def gate(c, silu, attn_ready):
        part = slice(4 * c, 4 * c + 4)
        dve.wait(silu, attn_ready)
        last = dve.did(vector.tensor_tensor(ffn[:, part, :], ffn[:, part, :], attn[:, part, :], ALU.mult))
        dve.wait(last)
        return dve.did(vector.tensor_tensor(x[:, part, :], x[:, part, :], ffn[:, part, :], ALU.add))

    def silu_of(c, ffn_ready):
        part = slice(4 * c, 4 * c + 4)
        act.wait(ffn_ready)
        return act.did(scalar.activation(ffn[:, part, :], ffn[:, part, :], ACT.Silu))

    def project_features(w, target, xnT_ready, weights):
        pe.wait(weights, *xnT_ready)
        act.wait(weights)
        for c in range(NC):
            i, bank, bank_free = accum.take()
            pe.wait(*bank_free)
            last = pe.did(tensor.matmul(bank, wqkvo[:, 0, w, :], xnT[:, c * BANK:(c + 1) * BANK], start=True, stop=True))
            act.wait(last)
            last = act.did(scalar.activation(target[:, c * BANK:(c + 1) * BANK], bank, ACT.Relu, bias=bqk[:, 0, w:w + 1]))
            accum.release(i, last)
        return last

    def value_products(L, xnT_ready, weights, chunks=range(NC)):
        for c in chunks:
            i, bank, free = accum.take()
            pe.wait(*free, weights, xnT_ready[c])
            for k in range(4):
                t = 4 * c + k
                last = tensor.matmul(bank[:, k * D:(k + 1) * D], xnT[:, t * P:(t + 1) * P], wqkvo[:, L, 2, :],
                                     start=True, stop=True)
            yield c, i, bank.rearrange("p (k d) -> p k d", d=D), pe.did(last)

    def bias_of(L, i):
        return bvo[:, L, i, :].unsqueeze(1).to_broadcast([P, 4, D])

    scope0 = [nc.sbuf_tensor(*s) for s in (
        ("qT", [P, T], FP32), ("kT", [P, T], FP32), ("v", [P, NT, D], FP32),
        ("causal", [P, S + (TPB - 1) * P], FP32), ("yT", [P, 2, P], FP32),
        ("scores", [P, 2, S], FP32), ("probs", [P, 3, S], FP32), ("probsT", [P, 2, S], FP32),
        ("l0_cols", [P, 3, NT], FP32))]
    qT, kT, v, causal, yT, scores, probs, probsT, l0_cols = [s.__enter__() for s in scope0]
    t = pool.did(gpsimd.memset(causal[:, :], 0.0))
    pool.wait(t)
    causal_done = pool.did(gpsimd.affine_select(
        out=causal[:, :], in_=causal[:, :], compare_op=ALU.is_ge, fill=-NEG, base=(TPB - 1) * P,
        pattern=[[-1, S + (TPB - 1) * P]], channel_multiplier=1))

    weights = load_layer_weights(0)
    routed_in = load_routed(0, ())
    zeroed = zero_routed(0)
    weights1 = load_layer_weights(1)
    guard_sem = Loads(nc, "ld_guard")
    guard_sem.did(sync.dma_start(head_sum[:, :], a["head_of"]))
    guard_in = guard_sem.did(sync.dma_start(far_limit[:, :], a["limits"]))
    normed = norm_apply(range(NC), norm_root(range(NC), norm_stats(range(NC), x_in)))
    xnT_ready = [flip_xn(c, normed[c]) for c in range(NC)]

    q_done = project_features(0, qT, xnT_ready, weights)
    k_done = project_features(1, kT, xnT_ready, weights)
    dve.wait(weights)
    for c, i, bank, t in value_products(0, xnT_ready, weights):
        dve.wait(t)
        part = slice(4 * c, 4 * c + 4)
        t = dve.did(vector.tensor_tensor(v[:, part, :], bank, bias_of(0, 0), ALU.add))
        accum.release(i, t)
        dve.wait(t)
        v_done = dve.did(vector.tensor_relu(v[:, part, :], v[:, part, :]))

    neg_max, row_sum, inv_sum = (l0_cols[:, n, :] for n in range(3))
    dve.wait(causal_done)
    pe.wait(v_done, q_done, k_done)
    scaled, exped, transposed, multiplied = {}, {}, {}, {}

    def l0_scores(t):
        b, i = divmod(t, TPB)
        s, pair, free = pairs.take()
        pe.wait(*free)
        for c in range(S // BANK):
            last = tensor.matmul(pair[:, c * BANK:(c + 1) * BANK], qT[:, t * P:(t + 1) * P],
                                 kT[:, b * S + c * BANK:b * S + (c + 1) * BANK], start=True, stop=True)
        last = pe.did(last)
        dve.wait(last, exped.get(t - 2))
        lo = (TPB - 1 - i) * P
        last = dve.did(vector.scalar_tensor_tensor(
            out=scores[:, t % 2, :], in0=pair, scalar=1.0 / float(np.sqrt(np.float32(D))), in1=causal[:, lo:lo + S],
            op0=ALU.mult, op1=ALU.add))
        pairs.release(s, last)
        dve.wait(last)
        scaled[t] = dve.did(vector.tensor_reduce(neg_max[:, t:t + 1], scores[:, t % 2, :], AX.X, ALU.max, negate=True))

    def l0_exp(t):
        act.wait(scaled[t], transposed.get(t - 3))
        exped[t] = act.did(scalar.activation(probs[:, t % 3, :], scores[:, t % 2, :], ACT.Exp,
                                             bias=neg_max[:, t:t + 1], accum_out=row_sum[:, t:t + 1]))

    probs_copied, y_copied, y_read, attn_done = {}, {}, {}, {}

    def l0_transposes(t):
        s, pair, free = pairs.take()
        pe.wait(*free, exped[t])
        for j in range(TPB):
            last = tensor.transpose(pair[:, j * P:(j + 1) * P], probs[:, t % 3, j * P:(j + 1) * P], ident[:, :])
        transposed[t] = pe.did(last)
        act.wait(transposed[t], multiplied.get(t - 2))
        probs_copied[t] = act.did(scalar.activation(probsT[:, t % 2, :], pair, ACT.Copy))
        pairs.release(s, probs_copied[t])

    def l0_values(t):
        b, i = divmod(t, TPB)
        s, bank, free = small.take()
        pe.wait(*free, probs_copied[t])
        for j in range(TPB):
            last = tensor.matmul(bank[:, 0:P], v[:, b * TPB + j, :], probsT[:, t % 2, j * P:(j + 1) * P],
                                 start=(j == 0), stop=(j == TPB - 1))
        multiplied[t] = pe.did(last)
        act.wait(multiplied[t], y_read.get(t - 2))
        y_copied[t] = act.did(scalar.activation(yT[:, t % 2, :], bank[:, 0:P], ACT.Copy))
        small.release(s, y_copied[t])

    def l0_output(t):
        s, bank, free = small.take()
        pe.wait(*free, y_copied[t])
        last = y_read[t] = pe.did(tensor.matmul(bank[:, 0:D], yT[:, t % 2, :], wqkvo[:, 0, 3, :], start=True, stop=True))
        dve.wait(exped[t])
        r = dve.did(vector.reciprocal(inv_sum[:, t:t + 1], row_sum[:, t:t + 1]))
        dve.wait(last, r)
        last = dve.did(vector.scalar_tensor_tensor(
            out=attn[:, t, :], in0=bank[:, 0:D], scalar=inv_sum[:, t:t + 1], in1=bvo[:, 0, 1, :],
            op0=ALU.mult, op1=ALU.add))
        small.release(s, last)
        dve.wait(last)
        attn_done[t // 4] = dve.did(vector.tensor_relu(attn[:, t, :], attn[:, t, :]))

    routed = {}

    def route_top_one():
        t = router_logits(0, xnT_ready, weights)
        yield
        mix_ready = yield from one_hot_of_max(logits, mix[:, :, 0:E], rcol, rt1, t)
        yield
        routed["placed"], routed["named"] = yield from dispatch(0, [mix[:, :, 0:E]], mix_ready)
        routed["scattered"] = scatter_rows(0, routed["placed"], normed.values(), zeroed)
        yield
        routed["mixT"] = yield from transpose_mix(E, mix_ready, ())

    def l0_attention(b, beside=None):
        tiles = range(b * TPB, (b + 1) * TPB)
        l0_scores(tiles[0])
        l0_exp(tiles[0])
        l0_scores(tiles[1])
        for t in tiles:
            l0_transposes(t)
            if t + 1 in tiles:
                l0_exp(t + 1)
            if t + 2 in tiles:
                l0_scores(t + 2)
            for step in (beside or {}).get(t - tiles[0], ()):
                step()
            l0_values(t)
            if t > tiles[0]:
                l0_output(t - 1)
        l0_output(tiles[-1])

    routing = route_top_one()
    l0_attention(0, {i: [lambda: "scattered" in routed or next(routing)] * 5 for i in range(TPB)})
    rows, rowsT, hidden, y_rows = (carve(0, shape) for shape in ffn_shapes)
    ffn_multiplied, stored = routed_ffn(0, ACT.Relu, (rows, rowsT, hidden, y_rows),
                                        routed["named"], routed["scattered"], routed_in, weights)
    run(routing)
    mixT_ready = routed["mixT"]
    biases_done = second_biases(0, mixT_ready, weights)
    picked_in = [gather_rows(0, 0, b, xn, stored, xnT_ready) for b in range(B)]
    routed_in1 = load_routed(1, (ffn_multiplied,))
    zeroed = zero_routed(1)
    shared_in = ld_shared.did(sync.dma_start(shared_w1[:, :], a["L1_W1"][E]))
    shared_in = ld_shared.did(sync.dma_start(shared_w2[:, :, :], a["L1_W2"][E].rearrange("(j p) d -> p j d", p=P)))

    x_done, normed, xnT_ready, silu, counted = {}, {}, {}, {}, {}
    ffn_done = {}

    def add_picked():
        for c in range(NC):
            dve.wait(picked_in[c * B // NC], biases_done)
            part = slice(4 * c, 4 * c + 4)
            ffn_done[c] = dve.did(vector.tensor_tensor(ffn[:, part, :], ffn[:, part, :], xn[:, part, :], ALU.add))

    def all_silu():
        for c in range(NC):
            silu[c] = silu_of(c, ffn_done[c])

    def end_layer0(chunks):
        for c in chunks:
            x_done[c] = gate(c, silu[c], attn_done[c])
        counted[chunks[-1]] = norm_stats(chunks, x_done)

    proj, rest, squares = (carve(1, [2, BANK]) for _ in range(3))
    parts = carve(1, [2, PARTS, S], BF16)
    st_split = [[Loads(nc, f"st_split_{w}{b}") for b in range(B)] for w in "qk"]
    split_stored, squares_read, split_read, split_in, split_done = [None] * 2, [None] * 2, [None] * 2, {}, {}
    st_alibi = Loads(nc, "st_alibi")
    for b in range(B):
        alibi_in = st_alibi.did(sync.dma_start(k_split[:, PROD_ROWS:, b * S:(b + 1) * S], a["alibi"].bitcast(BF16)))

    def project_and_split(w, c):
        cols = slice(c * BANK, (c + 1) * BANK)
        b = c // (NC // B)
        r = project_and_split.count % 2
        own = slice(c % (NC // B) * BANK, (c % (NC // B) + 1) * BANK)
        project_and_split.count += 1
        i, bank, free = accum.take()
        pe.wait(*free, xnT_ready[c], weights1)
        last = pe.did(tensor.matmul(bank, wqkvo[:, 1, w, :], xnT[:, cols], start=True, stop=True))
        act.wait(last, split_read[r])
        bias, scale = (bq_scaled[:, 0:1], HD ** -0.5) if w == 0 else (bqk[:, 1, 1:2], 1.0)
        projected = act.did(scalar.activation(proj[:, r, :], bank, ACT.Identity, bias=bias, scale=scale))
        accum.release(i, projected)
        act.wait(projected, split_stored[w])
        last = act.did(scalar.activation(parts[:, w, 0, own], proj[:, r, :], ACT.Copy))
        if w == 1 and (c + 1) % (NC // B) == 0:
            t = act.did(scalar.mul(last_key[:, b:b + 1], proj[:, r, BANK - 1:BANK], -1.0))
            act.wait(t)
        act.wait(squares_read[r])
        squared = act.did(scalar.activation(squares[:, r, :], proj[:, r, :], ACT.Square,
                                            bias=last_key[:, b:b + 1] if w == 1 else 0.0))
        dve.wait(last, split_stored[w])
        last = dve.did(vector.tensor_tensor(rest[:, r, :], proj[:, r, :], parts[:, w, 0, own], ALU.subtract))
        t = dve.did(vector.tensor_tensor(parts[:, w, 1, own], proj[:, r, :], parts[:, w, 0, own], ALU.subtract))
        dve.wait(last, t)
        last = dve.did(vector.tensor_tensor(parts[:, w, 2, own], rest[:, r, :], parts[:, w, 1, own], ALU.subtract))
        split_read[r] = last
        split_in[w, c] = last
        if (w, c ^ 1) in split_in:
            sp.wait(last, split_in[w, c ^ 1])
            for n in range(PARTS):
                for i in range(PARTS if w == 1 else 1):
                    row = (n * PARTS + i if w == 1 else n) * HD
                    t = st_split[w][b].did(sync.dma_start(
                        (q_split, k_split)[w][:, row:row + HD, b * S:(b + 1) * S], parts[:, w, n, :]))
            split_stored[w] = split_done[w, b] = t
        yield
        i, bank, free = accum.take()
        pe.wait(*free, squared, guard_in)
        squares_read[r] = pe.did(tensor.matmul(bank[0:H, :], head_sum[:, :], squares[:, r, :], start=True, stop=True))
        dve.wait(squares_read[r])
        last = dve.did(vector.tensor_reduce(norm_max[:, w, c:c + 1], bank[0:H, :], AX.X, ALU.max))
        accum.release(i, last)
        yield last

    project_and_split.count = 0
    in_split = []

    def split_next(*pairs_):
        for w, c in pairs_:
            piece = project_and_split(w, c)
            next(piece)
            in_split.append(piece)
            if len(in_split) > 1:
                next(in_split.pop(0))

    rooted = {}

    def root(chunks):
        rooted[chunks] = norm_root(chunks, counted[chunks[-1]])

    def apply_norm(chunks):
        normed.update(norm_apply(chunks, rooted[chunks]))

    def flip(c):
        xnT_ready[c] = flip_xn(c, normed[c])

    dve.wait(weights1)
    t = dve.did(vector.tensor_scalar(bq_scaled[:, :], bqk[:, 1, 0:1], HD ** -0.5, None, ALU.mult))
    act.wait(t)
    act.wait(ffn_multiplied, *stored)
    dve.wait(ffn_multiplied, *stored)
    first, second = range(0, 2), range(2, 4)
    l0_attention(1, {
        2: [add_picked],
        3: [all_silu],
        4: [lambda: end_layer0(first), lambda: root(first)],
        5: [lambda: apply_norm(first)],
        6: [lambda: flip(1), lambda: flip(0)],
        7: [lambda: split_next((1, 1)), lambda: split_next((1, 0)), lambda: end_layer0(range(2, 3))],
        })
    l0_done = attn_done[NC - 1]
    for s in reversed(scope0):
        s.__exit__(None, None, None)

    scope1 = []

    def scoped(name, shape, dt=FP32):
        scope1.append(nc.sbuf_tensor(name, shape, dt))
        return scope1[-1].__enter__()

    v_aug = scoped("v_aug", [P, NT, H, V_COLS])
    RING = 7
    AHEAD = 2
    FIRST = 4
    stacks = [[scoped(f"{w}_stack{n}", [P, S], BF16) for w in "qk"] for n in range(RING)]
    mergedT = scoped("mergedT", [P, 2, BANK])
    row_max = scoped("row_max", [P, 2, TPB])
    half_max = scoped("half_max", [P, 2])
    neg_row_max = scoped("neg_row_max", [P, 2, TPB], BF16)
    neg_row_maxT = scoped("neg_row_maxT", [TPB, 2, P], BF16)
    recips = scoped("recips", [P, 2, 4, 4])
    N_EXPS = 10
    exps = carve(2, [N_EXPS, BANK])
    heads_all = carve(2, [2 * 2, BANK]).rearrange("p (q g) n -> p q g n", q=2)
    merged = carve(2, [2, 4, D])
    v_flat = v_aug[:, :, :, :].rearrange("p t h c -> p (t h c)")
    hT = v_flat[:, 0:2 * FJ * BANK].rearrange("p (n j c) -> p n j c", n=2, j=FJ)
    picked1 = v_flat[:, 2 * FJ * BANK:2 * FJ * BANK + T].rearrange("p (t d) -> p t d", d=D)

    pool.wait(l0_done)
    dve.wait(l0_done)
    t = pool.did(gpsimd.memset(v_aug[:, :, :, HD:V_COLS], 0.0))
    pool.wait(t)
    v_ones = pool.did(gpsimd.memset(v_aug[:, :, :, HD:HD + 1], 1.0))
    units = [(b, h) for b in range(B) for h in range(H)]

    def column_group(h, qc):
        return (h + 2 * qc) % 4

    def load_stack(u, keys, ld):
        b, h = units[u]
        q_stack, k_stack = stacks[u % RING]
        k0 = S - keys
        ld.did(sync.dma_start(q_stack[0:PROD_ROWS, :],
                              q_split[h, :, b * S:(b + 1) * S].unsqueeze(0).to_broadcast([PARTS, PARTS * HD, S])))
        return ld.did(sync.dma_start(k_stack[0:PROD_ROWS + ALIBI_ROWS, k0:S], k_split[h, :, b * S + k0:(b + 1) * S]))

    def values(chunks):
        for c, i, bank, t in value_products(1, xnT_ready, weights1, chunks):
            dve.wait(t)
            for k in range(4):
                last = dve.did(vector.tensor_tensor(
                    v_aug[:, 4 * c + k, :, 0:HD], bank[:, k, :].rearrange("p (h d) -> p h d", d=HD),
                    bvo[:, 1, 0, :].rearrange("p (h d) -> p h d", d=HD), ALU.add))
            accum.release(i, last)
        return last

    const_sem = Loads(nc, "ld_const")
    sp.wait(l0_done)
    for n in range(RING):
        for w in range(2):
            consts_in = const_sem.did(sync.dma_start(
                stacks[n][w][PROD_ROWS:MAX_ROW + w, :], a["stack_rows"][w, 0:MAX_ROW + w - PROD_ROWS, :].bitcast(BF16)))

    sp.wait(consts_in)
    end_layer0(range(3, 4))
    split_next((0, 1))
    split_next((0, 0))
    sp.wait(alibi_in, *split_done.values())
    first_stacks = {u: load_stack(u, S, Loads(nc, f"ld_first_stack{u}")) for u in range(FIRST)}
    root(second)
    apply_norm(second)
    values(first)
    flip(3)
    flip(2)
    split_next((1, 3), (1, 2), (0, 3), (0, 2))
    widest = next(in_split.pop(0))

    dve.wait(widest, guard_in)
    last = dve.did(vector.tensor_reduce(
        batch_max[:, :, :], norm_max[:, :, :].rearrange("h w (b c) -> h w b c", b=B), AX.X, ALU.max))
    dve.wait(last)
    last = dve.did(vector.tensor_tensor(span[:, :], batch_max[:, 0, :], batch_max[:, 1, :], ALU.mult))
    dve.wait(last)
    last = dve.did(vector.tensor_reduce(worst[:, :], span[:, :], AX.X, ALU.max))
    dve.wait(last)
    last = dve.did(vector.tensor_tensor(worst[:, :], worst[:, :], far_limit[:, :], ALU.subtract))
    i, bank, bank_free = small.take()
    pe.wait(*bank_free, last)
    last = pe.did(tensor.transpose(bank[0:1, 0:H], worst[:, :], ident[0:H, 0:H]))
    dve.wait(last)
    last = dve.did(vector.tensor_reduce(worst_row[:, 0:1], bank[0:1, 0:H], AX.X, ALU.max))
    small.release(i, last)
    dve.wait(last)
    flagged = dve.did(vector.tensor_scalar(flag[:, :], worst_row[:, 0:1], 0.0, None, ALU.is_lt))

    v_done = values(second)

    def route_top_two():
        last = router_logits(1, xnT_ready.values(), weights1)
        yield
        dve.wait(last)
        last = dve.did(vector.tensor_reduce(rcol[:, :], logits[:, :, :], AX.X, ALU.max))
        dve.wait(last)
        last = dve.did(vector.tensor_tensor(logits[:, :, :], logits[:, :, :], over_experts(rcol), ALU.subtract))
        yield
        act.wait(last)
        last = act.did(scalar.activation(logits[:, :, :], logits[:, :, :], ACT.Exp))
        yield
        dve.wait(last)
        last = dve.did(vector.tensor_reduce(rcol[:, :], logits[:, :, :], AX.X, ALU.add))
        dve.wait(last)
        last = dve.did(vector.reciprocal(rcol[:, :], rcol[:, :]))
        yield
        dve.wait(last)
        last = dve.did(vector.tensor_tensor(logits[:, :, :], logits[:, :, :], over_experts(rcol), ALU.mult))
        last = yield from one_hot_of_max(logits, rt2[:, :, :], rcol, rt1, last)
        dve.wait(last)
        last = dve.did(vector.scalar_tensor_tensor(out=rt3[:, :, :], in0=rt2[:, :, :], scalar=-2.0,
                                                   in1=logits[:, :, :], op0=ALU.mult, op1=ALU.add))
        last = yield from one_hot_of_max(rt3, rt1[:, :, :], rcol2, rt1, last)
        placed, _ = yield from dispatch(1, [rt2[:, :, :], rt1[:, :, :]], last)
        scatter_rows(1, placed, normed.values(), zeroed)
        dve.wait(last, placed)
        last = dve.did(vector.tensor_tensor(rt1[:, :, :], rt1[:, :, :], rt2[:, :, :], ALU.add))
        last2 = dve.did(vector.tensor_tensor(rcol3[:, :], rcol[:, :], rcol2[:, :], ALU.add))
        yield
        dve.wait(last, last2)
        last = dve.did(vector.tensor_tensor(rt1[:, :, :], rt1[:, :, :], logits[:, :, :], ALU.mult))
        last2 = dve.did(vector.tensor_scalar(rcol3[:, :], rcol3[:, :], TOPK_EPS, None, ALU.add))
        dve.wait(last2)
        last2 = dve.did(vector.reciprocal(rcol3[:, :], rcol3[:, :]))
        yield
        dve.wait(last, last2)
        dve.did(vector.tensor_tensor(weight1[:, :], rcol[:, :], rcol3[:, :], ALU.mult))
        dve.did(vector.tensor_tensor(weight2[:, :], rcol2[:, :], rcol3[:, :], ALU.mult))
        dve.did(vector.memset(mix[:, :, E:E + 1], SHARED))
        mix_ready = dve.did(vector.tensor_tensor(mix[:, :, 0:E], rt1[:, :, :], over_experts(rcol3), ALU.mult))
        yield
        yield from transpose_mix(E + 1, mix_ready, ())

    def attention(arm, tiles, beside):
        stack_sem = [Loads(nc, f"ld_stack{n}{arm}") for n in range(RING)]
        max_sem = [Loads(nc, f"ld_max{n}{arm}") for n in range(RING)]
        stack_free = [() for _ in range(RING)]
        stack_in, max_in, maxed, max_flipped = dict(first_stacks), {}, {}, {}
        exp_slots = Slots([exps[:, n, :] for n in range(N_EXPS)])
        small.restart(banks[0:3])
        singles = Slots(banks[3:6])
        out_bank = {}
        heads_read, heads_in = [None] * 2, [None] * 2
        merged_read, mergedT_read, half_read = [None] * 2, [None] * 2, [None]
        head_merged, merged_flipped, merging = {}, {}, []

        def find_max(u):
            b, h = units[u]
            n, r = u % RING, u % 2
            q_stack, k_stack = stacks[n]
            keys = tiles[h] * P
            k0 = S - keys
            fit = max(1, BANK // keys)
            pieces = range(0, keys, BANK)

            def step(first, c):
                s, bank, free = small.take()
                pe.wait(stack_in[u], *free)
                w = min(BANK, keys - c)
                for m in range(fit):
                    i = first + m
                    last = tensor.matmul(bank[:, m * w:(m + 1) * w], q_stack[0:MAX_ROW, i * P:(i + 1) * P],
                                         k_stack[0:MAX_ROW, k0 + c:k0 + c + w], start=True, stop=True)
                last = pe.did(last)
                whole = len(pieces) == 1
                maxima = row_max[:, r, first:first + fit] if whole else half_max[:, c // BANK:c // BANK + 1]
                dve.wait(last, max_flipped.get(u - 2), half_read[0])
                last = dve.did(vector.tensor_reduce(
                    maxima, bank[:, 0:fit * w].rearrange("p (m k) -> p m k", k=w), AX.X, ALU.max))
                small.release(s, last)
                if c != pieces[-1]:
                    return
                if not whole:
                    dve.wait(last)
                    last = half_read[0] = dve.did(vector.tensor_reduce(
                        row_max[:, r, first:first + 1], half_max[:, :], AX.X, ALU.max))
                if first + fit >= TPB:
                    dve.wait(last)
                    maxed[u] = dve.did(vector.tensor_scalar(neg_row_max[:, r, :], row_max[:, r, :], -1.0, None, ALU.mult))

            return [lambda first=first, c=c: step(first, c) for first in range(0, TPB, fit) for c in pieces]

        def place_max(u):
            n, r = u % RING, u % 2
            s, bank, free = small.take()
            pe.wait(*free, maxed[u])
            flipped = bank.bitcast(BF16)[0:TPB, 0:P]
            last = max_flipped[u] = pe.did(tensor.transpose(flipped, neg_row_max[:, r, :], ident_b[:, :]))
            dve.wait(last, max_in.get(u - 2))
            last = dve.did(vector.tensor_copy(neg_row_maxT[:, r, :], flipped))
            small.release(s, last)
            sp.wait(last)
            max_in[u] = max_sem[n].did(sync.dma_start(stacks[n][0][MAX_ROW:MAX_ROW + 1, :], neg_row_maxT[:, r, :]))

        quads = []

        def attend(p, between):
            b, h0 = units[2 * p]
            kept = range(TPB - tiles[h0], TPB)
            for j in kept:
                quad = []
                for u in (2 * p, 2 * p + 1):
                    q_stack, k_stack = stacks[u % RING]
                    for qc in range(S // BANK):
                        s, bank, free = singles.take()
                        pe.wait(*free, max_in[u])
                        last = pe.did(tensor.matmul(
                            bank, k_stack[0:MAX_ROW + 1, j * P:(j + 1) * P],
                            q_stack[0:MAX_ROW + 1, qc * BANK:(qc + 1) * BANK], start=True, stop=True))
                        es, p_buf, p_free = exp_slots.take()
                        act.wait(last, *p_free)
                        t = act.did(scalar.activation(p_buf, bank, ACT.Exp))
                        singles.release(s, t)
                        quad.append((u, qc, j, es, p_buf, t))
                        between()
                quads.append(quad)
                if len(quads) > 1:
                    multiply(quads.pop(0))
                    if j == kept[0]:
                        load_more(2 * p)
                between()

        def multiply(quad):
            pe.wait(quad[-1][-1])
            for u, qc, j, es, p_buf, t in quad:
                b, h = units[u]
                first, final = j == TPB - tiles[h], j == TPB - 1
                if h % 4 == 0 and first:
                    out_bank[qc] = accum.take()
                    pe.wait(*out_bank[qc][2])
                at = column_group(h, qc) * V_COLS
                last = tensor.matmul(out_bank[qc][1][at:at + V_COLS, :], v_aug[:, b * TPB + j, h, :], p_buf,
                                     start=first, stop=final, tile_position=(0, at))
            last = pe.did(last)
            for u, qc, j, es, p_buf, t in quad:
                exp_slots.release(es, last)
                stack_free[u % RING] = (last,)
            if h % 4 == 3 and final:
                g = h // 4
                for qc in range(S // BANK):
                    slot, bank, _ = out_bank[qc]
                    act.wait(last, heads_read[qc])
                    heads_in[qc] = act.did(scalar.activation(heads_all[:, qc, g % 2, :], bank, ACT.Copy))
                    accum.release(slot, heads_in[qc])
                    merging.append(lambda qc=qc: merge_heads(qc, g))
                if h == H - 1:
                    merging.extend(lambda qc=qc: flip_merged(qc) for qc in range(S // BANK))
                    merging.extend(lambda qc=qc: project(b, qc) for qc in range(S // BANK))

        def merge_heads(qc, g):
            s, bank, free = small.take()
            pe.wait(*free, heads_in[qc])
            for k in range(4):
                last = tensor.transpose(bank[:, k * P:(k + 1) * P], heads_all[:, qc, g % 2, k * P:(k + 1) * P], ident[:, :])
            last = heads_read[qc] = pe.did(last)
            by_head = bank.rearrange("p (k h c) -> p k h c", k=4, c=V_COLS)
            dve.wait(last, head_merged.get(qc))
            last = dve.did(vector.reciprocal(recips[:, qc, :, :], by_head[:, :, :, HD]))
            dve.wait(last, merged_read[qc])
            to = merged[:, qc, :, g * 4 * HD:(g + 1) * 4 * HD].rearrange("p k (h d) -> p k h d", d=HD)
            for h in (0, 2):
                at = column_group(h, qc)
                last = dve.did(vector.tensor_tensor(
                    to[:, :, h:h + 2, :], by_head[:, :, at:at + 2, 0:HD],
                    recips[:, qc, :, at:at + 2].unsqueeze(3).to_broadcast([P, 4, 2, HD]), ALU.mult))
            small.release(s, last)
            head_merged[qc] = last

        def flip_merged(qc):
            s, bank, free = small.take()
            pe.wait(*free, head_merged[qc])
            for k in range(4):
                last = tensor.transpose(bank[:, k * P:(k + 1) * P], merged[:, qc, k, :], ident[:, :])
            last = merged_read[qc] = pe.did(last)
            act.wait(last, mergedT_read[qc])
            merged_flipped[qc] = act.did(scalar.activation(mergedT[:, qc, :], bank, ACT.Copy))
            small.release(s, merged_flipped[qc])

        def project(b, qc):
            s, bank, free = small.take()
            pe.wait(*free, merged_flipped[qc])
            for k in range(4):
                last = tensor.matmul(bank[:, k * D:(k + 1) * D], mergedT[:, qc, k * P:(k + 1) * P], wqkvo[:, 1, 3, :],
                                     start=True, stop=True)
            last = mergedT_read[qc] = pe.did(last)
            dve.wait(last)
            t0 = b * TPB + 4 * qc
            last = dve.did(vector.tensor_tensor(attn[:, t0:t0 + 4, :], bank.rearrange("p (k d) -> p k d", d=D), bias_of(1, 1), ALU.add))
            small.release(s, last)

        def load_more(behind):
            for u in range(len(stack_in), min(behind + RING, len(units))):
                sp.wait(*stack_free[u % RING])
                stack_in[u] = load_stack(u, tiles[units[u][1]] * P, stack_sem[u % RING])

        assert all(tiles[h] == tiles[h + 1] for h in range(0, H, 2))
        load_more(0)
        search_steps = []
        for u in range(len(units)):
            steps = find_max(u)
            if u > 0:
                steps.insert(2, lambda u=u: place_max(u - 1))
            search_steps.append(steps)
        search_steps.append([lambda: place_max(len(units) - 1)])
        upto = np.cumsum([0] + [len(steps) for steps in search_steps])
        searches = [step for steps in search_steps for step in steps]
        done = [0]

        def search_to(end):
            while done[0] < min(end, len(searches)):
                searches[done[0]]()
                done[0] += 1

        search_to(upto[3] + AHEAD)
        for p in range(len(units) // 2):
            begin, end = done[0], upto[min(2 * p + 5, len(units) + 1)] + AHEAD
            places, n_places = [0], 5 * tiles[units[2 * p][1]]

            def between():
                places[0] += 1
                search_to(begin + (end - begin) * places[0] // n_places)
                if places[0] % 2 == 0:
                    if merging:
                        merging.pop(0)()
                    else:
                        next(beside, None)

            attend(p, between)
        multiply(quads.pop(0))
        for step in merging:
            step()
        run(beside)
        small.restart(banks[0:2])

    sp.wait(*split_done.values())
    pe.wait(consts_in, v_ones, v_done)
    rejoin("_l1")
    near = nc.values_load(flag[0:1, 0:1], min_val=0, max_val=1)
    with nc.If(near > 0):
        rejoin("_near", barrier=False)
        attention("_near", [near_tiles(h) for h in range(H)], route_top_two())
    with nc.Else():
        rejoin("_far", barrier=False)
        st_rows[1].count = 0
        attention("_far", [TPB] * H, route_top_two())
    rejoin("_end")
    scattered = (st_rows[1].sem, st_rows[1].count)
    rows, rowsT, hidden, y_rows = (carve(3, shape) for shape in ffn_shapes)
    _, stored = routed_ffn(1, ACT.Silu, (rows, rowsT, hidden, y_rows), None, scattered, routed_in1, weights1)
    picked_in = {(b, k): gather_rows(1, k, b, (picked1, xn)[k], stored, ()) for b in range(B) for k in range(2)}
    biases_done = second_biases(1, None, weights1)
    silu = {}

    def finish(c):
        last = gate(c, silu[c], None)
        sp.wait(last)
        part = slice(4 * c, 4 * c + 4)
        st_out.did(sync.dma_start(out.rearrange("b (t p) d -> p (b t) d", p=P)[:, part, :], x[:, part, :]))

    def combine(c):
        for k, (picked, column) in enumerate(((picked1, weight1), (xn, weight2))):
            dve.wait(picked_in[c * B // NC, k], last_tick(dve))
            for t in range(4 * c, 4 * c + 4):
                last = dve.did(vector.scalar_tensor_tensor(
                    out=ffn[:, t, :], in0=picked[:, t, :], scalar=column[:, t:t + 1], in1=ffn[:, t, :],
                    op0=ALU.mult, op1=ALU.add))
        silu[c] = silu_of(c, last)

    def behind(c):
        if c > 0:
            combine(c - 1)
        if c > 1:
            finish(c - 2)

    shared_ffn(hT, None, weights1, shared_in, biases_done, behind)
    combine(NC - 1)
    finish(NC - 2)
    finish(NC - 1)
    sync.wait_ge(st_out.sem, st_out.count)
    for s in reversed(scope1):
        s.__exit__(None, None, None)


def split_constant(values):
    parts, rest = [], values.astype(np.float32)
    for _ in range(PARTS):
        part = (rest.view(np.uint32) & np.uint32(0xFFFF0000)).view(np.float32)
        parts.append((part.view(np.uint32) >> 16).astype(np.uint16))
        rest = rest - part
    return np.stack(parts)


def kernel(**inputs):
    import concourse.bacc as bacc
    from concourse.bass_utils import run_bass_kernel_spmd

    g = {k: np.asarray(v) for k, v in inputs.items()}
    arrays = {k: g[k] for k in g if "_attn_" in k}
    arrays["L0_ffn_br"] = g["L0_ffn_br"]
    arrays["L0_router"] = g["L0_ffn_Wr"].T
    arrays["L0_W1"] = g["L0_ffn_W1"].transpose(0, 2, 1)
    arrays["L0_W2"] = g["L0_ffn_W2"].transpose(0, 2, 1)
    arrays["L0_b1"], arrays["L0_b2"] = g["L0_ffn_b1"], g["L0_ffn_b2"]
    arrays["L1_router"] = g["L1_ffn_Wg"]
    for w in ("W1", "W2", "b1", "b2"):
        arrays[f"L1_{w}"] = np.concatenate([g[f"L1_ffn_{w}"], g[f"L1_ffn_{w[0]}s{w[1]}"][None]])
    for L in range(2):
        arrays[f"L{L}_b1"] = arrays[f"L{L}_b1"].reshape(E + L, FJ, P).transpose(2, 0, 1)
    slopes = 1.0 / 2.0 ** (np.arange(H, dtype=np.float32) / H)
    rel = slopes[:, None].astype(np.float32) * (np.arange(S, dtype=np.float32) - (S - 1))[None, :]
    arrays["alibi"] = np.ascontiguousarray(split_constant(rel).transpose(1, 0, 2))
    stack_rows = np.zeros((2, MAX_ROW + 1 - PROD_ROWS, S), np.float32)
    stack_rows[0, 0:ALIBI_ROWS] = 1.0
    stack_rows[1, -1] = 1.0
    arrays["stack_rows"] = split_constant(stack_rows)[0]
    arrays["head_of"] = np.kron(np.eye(H, dtype=np.float32), np.ones((HD, 1), np.float32))
    ids = np.arange(MAX_BLOCKS, dtype=np.float32)
    arrays["ids"] = np.broadcast_to(np.stack([ids, P * ids]), (P, 2, MAX_BLOCKS))
    arrays["limits"] = np.array([[(slope(h) * near_tiles(h) * P - UNDERFLOW) ** 2] for h in range(H)], np.float32)
    arrays = {k: np.ascontiguousarray(v) for k, v in arrays.items()}

    nc = bacc.Bacc("TRN2", target_bir_lowering=False, num_devices=1)
    aps = {k: nc.dram_tensor(k, v.shape, mybir.dt.from_np(v.dtype), kind="ExternalInput").ap() for k, v in arrays.items()}
    out = nc.dram_tensor("y", (B, S, D), FP32, kind="ExternalOutput").ap()
    build(nc, aps, out)
    r = run_bass_kernel_spmd(nc, [arrays], core_ids=[0])
    return r.results[0]["y"]
```
